# Optimizing a Trainium2 kernel written in Bass

```python
import numpy as np
import jax
import jax.numpy as jnp

def _softmax(x, axis=-1):
    return jax.nn.softmax(x, axis=axis)

def _gelu(x):
    return jax.nn.gelu(x, approximate=True)

def _silu(x):
    return jax.nn.silu(x)

def _sigmoid(x):
    return jax.nn.sigmoid(x)

def _layernorm(x, axis=-1, eps=1e-05):
    m = jnp.mean(x, axis=axis, keepdims=True)
    v = jnp.var(x, axis=axis, keepdims=True)
    return (x - m) / jnp.sqrt(v + eps)

def _scatter_add(tgt, idx, src, axis=0):
    return tgt.at[idx].add(src)

def _segment_sum(src, seg, n):
    return jax.ops.segment_sum(src, seg, n)
kernel_name = 'mk_macaron_d1_jaxref_r8_23a6ed'

def setup_inputs(seed: int=0):
    np.random.seed(seed)
    _w = jnp.asarray

    def _L0_attn_setup():
        import jax, jax.numpy as jnp
        import numpy as np
        DIM = 128
        QK = 128
        HID = 256
        B, N = (4, 256)
        EPS = 1e-05
        key = jax.random.key(seed)
        ks = jax.random.split(key, 8)
        std = 0.02
        return {'x': jax.random.normal(ks[0], (B, N, DIM), jnp.float32), 'ln_scale': jnp.ones((DIM,), jnp.float32), 'ln_bias': jnp.zeros((DIM,), jnp.float32), 'W_hidden': jax.random.normal(ks[1], (DIM, 2 * HID), jnp.float32) * std, 'b_hidden': jnp.zeros((2 * HID,), jnp.float32), 'W_qk': jax.random.normal(ks[2], (DIM, QK), jnp.float32) * std, 'b_qk': jnp.zeros((QK,), jnp.float32), 'os_weight': jax.random.normal(ks[3], (2, QK), jnp.float32) * std, 'os_bias': jnp.zeros((2, QK), jnp.float32), 'W_out': jax.random.normal(ks[4], (HID, DIM), jnp.float32) * std, 'b_out': jnp.zeros((DIM,), jnp.float32)}
    _L0_attn_in = _L0_attn_setup()

    def _L0_ffn_setup():
        import jax, jax.numpy as jnp
        import numpy as np
        from jax import lax
        D = 128
        H = 176
        E = 8
        K = 2
        ROUTER_SCALE = 1.0

        def _expert(x, w1, b1, w3, b3, w2, b2):
            h = jax.nn.silu((x @ w1 + b1) * (x @ w3 + b3))
            return h @ w2 + b2
        key = jax.random.key(seed)
        ks = jax.random.split(key, 16)
        s = 0.02
        inp = {'x': jax.random.normal(ks[0], (2, 256, D), dtype=jnp.float32), 'gate_w': jax.random.normal(ks[1], (E, D), dtype=jnp.float32) * s, 'gate_b': jax.random.normal(ks[2], (E,), dtype=jnp.float32) * s, 'w1': jax.random.normal(ks[3], (E, D, H), dtype=jnp.float32) * s, 'b1': jax.random.normal(ks[4], (E, H), dtype=jnp.float32) * s, 'w3': jax.random.normal(ks[5], (E, D, H), dtype=jnp.float32) * s, 'b3': jax.random.normal(ks[6], (E, H), dtype=jnp.float32) * s, 'w2': jax.random.normal(ks[7], (E, H, D), dtype=jnp.float32) * s, 'b2': jax.random.normal(ks[8], (E, D), dtype=jnp.float32) * s, 'sw1': jax.random.normal(ks[9], (D, H), dtype=jnp.float32) * s, 'sb1': jax.random.normal(ks[10], (H,), dtype=jnp.float32) * s, 'sw3': jax.random.normal(ks[11], (D, H), dtype=jnp.float32) * s, 'sb3': jax.random.normal(ks[12], (H,), dtype=jnp.float32) * s, 'sw2': jax.random.normal(ks[13], (H, D), dtype=jnp.float32) * s, 'sb2': jax.random.normal(ks[14], (D,), dtype=jnp.float32) * s}
        return inp
    _L0_ffn_in = _L0_ffn_setup()
    _d = {'L0_attn_x': _L0_attn_in['x'], 'L0_attn_ln_scale': _L0_attn_in['ln_scale'], 'L0_attn_ln_bias': _L0_attn_in['ln_bias'], 'L0_attn_W_hidden': _L0_attn_in['W_hidden'], 'L0_attn_b_hidden': _L0_attn_in['b_hidden'], 'L0_attn_W_qk': _L0_attn_in['W_qk'], 'L0_attn_b_qk': _L0_attn_in['b_qk'], 'L0_attn_os_weight': _L0_attn_in['os_weight'], 'L0_attn_os_bias': _L0_attn_in['os_bias'], 'L0_attn_W_out': _L0_attn_in['W_out'], 'L0_attn_b_out': _L0_attn_in['b_out'], 'L0_ffn_gate_w': _L0_ffn_in['gate_w'], 'L0_ffn_gate_b': _L0_ffn_in['gate_b'], 'L0_ffn_w1': _L0_ffn_in['w1'], 'L0_ffn_b1': _L0_ffn_in['b1'], 'L0_ffn_w3': _L0_ffn_in['w3'], 'L0_ffn_b3': _L0_ffn_in['b3'], 'L0_ffn_w2': _L0_ffn_in['w2'], 'L0_ffn_b2': _L0_ffn_in['b2'], 'L0_ffn_sw1': _L0_ffn_in['sw1'], 'L0_ffn_sb1': _L0_ffn_in['sb1'], 'L0_ffn_sw3': _L0_ffn_in['sw3'], 'L0_ffn_sb3': _L0_ffn_in['sb3'], 'L0_ffn_sw2': _L0_ffn_in['sw2'], 'L0_ffn_sb2': _L0_ffn_in['sb2']}
    _x0 = _d['L0_attn_x']
    _d['L0_attn_x'] = jax.random.normal(jax.random.fold_in(jax.random.key(seed), 1), (8, 1024, 128), dtype=_x0.dtype)
    del _x0
    return _d

def reference(L0_attn_x, L0_attn_ln_scale, L0_attn_ln_bias, L0_attn_W_hidden, L0_attn_b_hidden, L0_attn_W_qk, L0_attn_b_qk, L0_attn_os_weight, L0_attn_os_bias, L0_attn_W_out, L0_attn_b_out, L0_ffn_gate_w, L0_ffn_gate_b, L0_ffn_w1, L0_ffn_b1, L0_ffn_w3, L0_ffn_b3, L0_ffn_w2, L0_ffn_b2, L0_ffn_sw1, L0_ffn_sb1, L0_ffn_sw3, L0_ffn_sb3, L0_ffn_sw2, L0_ffn_sb2):

    def _L0_attn_ref(x, ln_scale, ln_bias, W_hidden, b_hidden, W_qk, b_qk, os_weight, os_bias, W_out, b_out):
        import jax, jax.numpy as jnp
        import numpy as np
        DIM = 128
        QK = 128
        HID = 256
        B, N = (4, 256)
        EPS = 1e-05
        n = x.shape[1]
        mu = jnp.mean(x, axis=-1, keepdims=True)
        var = jnp.mean(jnp.square(x - mu), axis=-1, keepdims=True)
        xn = (x - mu) / jnp.sqrt(var + EPS) * ln_scale + ln_bias
        hid = jax.nn.silu(xn @ W_hidden + b_hidden)
        v, gate = (hid[..., :HID], hid[..., HID:])
        qk = jax.nn.silu(xn @ W_qk + b_qk)
        qk2 = qk[..., None, :] * os_weight + os_bias
        q, k = (qk2[..., 0, :], qk2[..., 1, :])
        sim = jnp.einsum('bid,bjd->bij', q, k) / n
        attn = jnp.square(jax.nn.relu(sim))
        out = jnp.einsum('bij,bjd->bid', attn, v)
        out = out * gate
        return out @ W_out + b_out

    def _L0_ffn_ref(x, gate_w, gate_b, w1, b1, w3, b3, w2, b2, sw1, sb1, sw3, sb3, sw2, sb2):
        import jax, jax.numpy as jnp
        import numpy as np
        from jax import lax
        D = 128
        H = 176
        E = 8
        K = 2
        ROUTER_SCALE = 1.0

        def _expert(x, w1, b1, w3, b3, w2, b2):
            h = jax.nn.silu((x @ w1 + b1) * (x @ w3 + b3))
            return h @ w2 + b2
        shape = x.shape
        xf = x.reshape(-1, D)
        T = xf.shape[0]
        scores = jax.nn.softmax(xf @ gate_w.T, axis=-1)
        biased = scores + gate_b
        _, idx = lax.top_k(biased, K)
        w = jnp.take_along_axis(scores, idx, axis=-1) * ROUTER_SCALE
        rw = jnp.zeros((T, E), dtype=xf.dtype).at[jnp.arange(T)[:, None], idx].add(w)
        h = jax.nn.silu((jnp.einsum('td,edh->teh', xf, w1) + b1) * (jnp.einsum('td,edh->teh', xf, w3) + b3))
        oe = jnp.einsum('teh,ehd->ted', h, w2) + b2
        y = jnp.einsum('te,ted->td', rw, oe)
        z = _expert(xf, sw1, sb1, sw3, sb3, sw2, sb2)
        return (y + z).reshape(shape)
    x = L0_attn_x
    x = x + 0.5 * _L0_ffn_ref(_layernorm(x, axis=-1), L0_ffn_gate_w, L0_ffn_gate_b, L0_ffn_w1, L0_ffn_b1, L0_ffn_w3, L0_ffn_b3, L0_ffn_w2, L0_ffn_b2, L0_ffn_sw1, L0_ffn_sb1, L0_ffn_sw3, L0_ffn_sb3, L0_ffn_sw2, L0_ffn_sb2)
    x = x + _L0_attn_ref(_layernorm(x, axis=-1), L0_attn_ln_scale, L0_attn_ln_bias, L0_attn_W_hidden, L0_attn_b_hidden, L0_attn_W_qk, L0_attn_b_qk, L0_attn_os_weight, L0_attn_os_bias, L0_attn_W_out, L0_attn_b_out)
    x = x + 0.5 * _L0_ffn_ref(_layernorm(x, axis=-1), L0_ffn_gate_w, L0_ffn_gate_b, L0_ffn_w1, L0_ffn_b1, L0_ffn_w3, L0_ffn_b3, L0_ffn_w2, L0_ffn_b2, L0_ffn_sw1, L0_ffn_sb1, L0_ffn_sw3, L0_ffn_sb3, L0_ffn_sw2, L0_ffn_sb2)
    return x

_drawn_inputs = setup_inputs


def setup_inputs(seed=0):
    import zlib

    import numpy as np

    out = dict(_drawn_inputs(seed))
    spreads = {'L0_attn_ln_scale': (1.0, 0.2),
     'L0_attn_ln_bias': (0.0, 0.1),
     'L0_attn_b_hidden': (0.0, 0.1),
     'L0_attn_b_qk': (0.0, 0.1),
     'L0_attn_os_bias': (0.0, 0.1),
     'L0_attn_b_out': (0.0, 0.1)}
    factors = {'L0_ffn_gate_w': 8.0,
     'L0_ffn_gate_b': 8.0,
     'L0_ffn_w1': 8.0,
     'L0_ffn_b1': 8.0,
     'L0_ffn_w3': 8.0,
     'L0_ffn_b3': 8.0,
     'L0_ffn_w2': 8.0,
     'L0_ffn_b2': 8.0,
     'L0_ffn_sw1': 8.0,
     'L0_ffn_sb1': 8.0,
     'L0_ffn_sw3': 8.0,
     'L0_ffn_sb3': 8.0,
     'L0_ffn_sw2': 8.0,
     'L0_ffn_sb2': 2.864}
    for name, (base, spread) in spreads.items():
        noise = np.random.default_rng([zlib.crc32(name.encode()), seed]).standard_normal(out[name].shape)
        drawn = base * np.exp(spread * noise) if base else spread * noise
        out[name] = jnp.asarray(drawn.astype(out[name].dtype))
    for name, factor in factors.items():
        out[name] = (out[name] * factor).astype(out[name].dtype)
    return out
```

```python
from contextlib import ExitStack

import numpy as np

import concourse.bass as bass
from concourse import mybir

F32 = mybir.dt.float32
F32R = mybir.dt.float32r
I32 = mybir.dt.int32
ALU = mybir.AluOpType
ACT = mybir.ActivationFunctionType
AX = mybir.AxisListType

B, N, D = 8, 1024, 128
E, H, HID = 8, 176, 256
P = 128
HALF = N // 2
TT = HALF // P
NR = E * H // P
NBL = -(-(E + 1) * H // P)
HW = NBL * P
KT = N // P
RING = 2 + TT + 4 + 2 * KT
SIM0 = RING - 2 * KT
LAG = 3
NORM_STEPS, ROUTE_STEPS, RANK_STEPS = 14, 11, 5
EPS = 1e-5

C_B1, C_B3 = 0, NBL
C_SB2 = 2 * NBL
C_LNS, C_LNB, C_BQK, C_BG = C_SB2 + 1, C_SB2 + 2, C_SB2 + 3, C_SB2 + 4
C_QW, C_KW, C_QB, C_KB = C_BG + 2, C_BG + 3, C_BG + 4, C_BG + 5
C_BO = C_BG + 6
C_GB = C_BO + 1
NCOL = C_GB + E


class Count:

    def __init__(self, first, step=0, turn=None):
        self.first, self.step, self.turn = first, step, turn

    def __add__(self, k):
        return Count(self.first + k, self.step, self.turn)

    def __sub__(self, k):
        return self + -k

    def __mul__(self, k):
        return Count(self.first * k, self.step * k, self.turn)

    @property
    def due(self):
        return self.turn is not None or self.first > 0

    @property
    def value(self):
        assert self.first > 0
        return self.first if self.turn is None else self.turn * self.step + self.first

    def mod(self, m):
        assert self.step % m == 0
        return self.first % m


class Chunk:

    def __init__(self, q, r, b, half, ffn):
        self.q, self.r, self.b, self.half, self.ffn = q, r, b, half, ffn


class Norm:

    def __init__(self, u, kind, source, b, half, r=None, q=None):
        self.u, self.kind, self.source, self.b, self.half, self.r, self.q = u, kind, source, b, half, r, q


def phases_before():
    c = [Chunk(Count(k), Count(k), Count(0), k, 1) for k in range(2)]
    first = Norm(Count(0), "ffn", "xin", Count(0), 0, Count(0), Count(-1))
    second = Norm(Count(1), "ffn", "xin", Count(0), 1, Count(1), Count(0))
    att = [Norm(Count(2 + h), "att", "xa", Count(0), h) for h in range(2)]
    following = Norm(Count(4), "ffn", "xin", Count(1), 0, Count(2), Count(1))
    return c, first, second, att, following


def phases_of_turn(turn):
    q, u = Count(2, 4, turn), Count(5, 6, turn)
    b, last = Count(1, 1, turn), Count(0, 1, turn)
    c = [Chunk(q + k, q + k, b if k < 2 else last, k % 2, 1 if k < 2 else 2) for k in range(4)]
    preps = [
        [Norm(u, "ffn", "xin", b, 1, q + 1, q)],
        [Norm(u + 1, "ffn", "xb", last, 0, q + 2, q + 1)],
        [Norm(u + 2, "ffn", "xb", last, 1, q + 3, q + 2)],
        [Norm(u + 3, "att", "xa", b, 0), Norm(u + 4, "att", "xa", b, 1)],
    ]
    following = Norm(u + 5, "ffn", "xin", b + 1, 0, q + 4, q + 3)
    return c, preps, b, following


def phases_after():
    q, u, b = 4 * B - 2, 6 * B - 1, Count(B - 1)
    c = [Chunk(Count(q + k), Count(q + 1 + k), b, k, 2) for k in range(2)]
    first = Norm(Count(u), "ffn", "xb", b, 0, Count(q + 1), Count(q))
    second = Norm(Count(u + 1), "ffn", "xb", b, 1, Count(q + 2), Count(q))
    return c, first, second


def build(nc, x, cols, consts, sel, w1, w3, w2, wsmall, b2, bv, out):
    with ExitStack() as ctx:
        def sb(name, shape, dt=F32):
            return ctx.enter_context(nc.sbuf_tensor(name, shape, dt))

        def sem(name):
            return ctx.enter_context(nc.semaphore(name))

        ring = [ctx.enter_context(nc.psum_tensor(f"ring{k}", [P, HALF], F32)) for k in range(4)]
        rwb = ctx.enter_context(nc.psum_tensor("rwb", [P, HALF], F32))
        y = ctx.enter_context(nc.psum_tensor("y", [P, HALF], F32))
        tn = ctx.enter_context(nc.psum_tensor("tn", [P, HALF], F32))
        tp = ctx.enter_context(nc.psum_tensor("tp", [P, HALF], F32))

        w1_h, w1_l = sb("w1_h", [P, HW], F32R), sb("w1_l", [P, HW], F32R)
        w3_h, w3_l = sb("w3_h", [P, HW], F32R), sb("w3_l", [P, HW], F32R)
        w2_h, w2_l = sb("w2_h", [P, HW], F32R), sb("w2_l", [P, HW], F32R)
        WS = 2 * HID + D + 2 * D + E
        ws_h, ws_l = sb("ws_h", [P, WS], F32R), sb("ws_l", [P, WS], F32R)
        O_QK, O_OUT, O_GW = 2 * HID, 2 * HID + D, 2 * HID + 3 * D
        sel_sb = sb("sel_sb", [2 * E, E * H], F32R)
        b2_f = sb("b2_f", [3 * E, D])
        b2_h, b2_lo = sb("b2_h", [3 * E, D], F32R), sb("b2_lo", [3 * E, D], F32R)
        bv_f = sb("bv_f", [2, HID])
        bv_h, bv_lo = sb("bv_h", [2, HID], F32R), sb("bv_lo", [2, HID], F32R)
        ones = sb("ones", [2, P], F32R)
        col = sb("col", [P, NCOL])
        hb2 = sb("hb2", [P, 1])
        const = sb("const", [P, P + E * E + P])
        ident, before = const[:, 0:P], const[:, P:P + E * E]
        ones_f = const[0:2, P + E * E:]

        xin, xa, xb = sb("xin", [P, KT * D]), sb("xa", [P, KT * D]), sb("xb", [P, KT * D])
        res = sb("res", [P, KT * D])
        st, mv = sb("st", [P, TT, 6]), sb("mv", [P, TT, 2])
        vv, ri, t1, t2 = sb("vv", [P, TT]), sb("ri", [P, TT], I32), sb("t1", [P, TT]), sb("t2", [P, TT])
        xn = sb("xn", [P, HALF])
        xt_h = [sb(f"xt_h{k}", [P, HALF], F32R) for k in range(2)]
        xt_l = [sb(f"xt_l{k}", [P, HALF], F32R) for k in range(2)]
        mx, sm, rc = sb("mx", [P, TT]), sb("sm", [P, TT]), sb("rc", [P, TT])
        lg, ex, sc, bi = (sb(k, [P, TT, E]) for k in ("lg", "ex", "sc", "bi"))
        diff = sb("diff", [P, TT, E * E])
        gt, eq = sb("gt", [P, TT, E * E]), sb("eq", [P, TT, E * E])
        rank, rw = sb("rank", [P, TT, E]), sb("rw", [P, TT, E])
        rwh = sb("rwh", [P, TT, E], F32R)
        rw3 = sb("rw3", [P, TT, P])
        rwt = [sb(f"rwt{k}", [3 * E, HALF], F32R) for k in range(2)]
        u = [sb(f"u{k}", [P, HALF]) for k in range(2)]
        g = [sb(f"g{k}", [P, HALF]) for k in range(4)]
        p = [sb(f"p{k}", [P, HALF]) for k in range(2)]
        p_h = [sb(f"p_h{k}", [P, HALF], F32R) for k in range(4)]
        p_l = [sb(f"p_l{k}", [P, HALF], F32R) for k in range(4)]
        ys = sb("ys", [P, HALF])
        axf = sb("axf", [P, HALF])
        ax_h, ax_l = sb("ax_h", [P, N], F32R), sb("ax_l", [P, N], F32R)
        scratch = sb("scratch", [P, 5 * N])
        qkf, kqt = scratch[:, 0:N], scratch[:, N:2 * N]
        vf, gate = scratch[:, 2 * N:3 * N], scratch[:, 3 * N:5 * N]
        k_h, k_l = sb("k_h", [P, N], F32R), sb("k_l", [P, N], F32R)
        q_h, q_l = sb("q_h", [P, N], F32R), sb("q_l", [P, N], F32R)
        v_h, v_l = sb("v_h", [P, KT * HID], F32R), sb("v_l", [P, KT * HID], F32R)
        o_f, o_h, o_l = sb("o_f", [P, N]), sb("o_h", [P, N], F32R), sb("o_l", [P, N], F32R)

        w_loaded = [sem(f"w_loaded{k}") for k in range(9)]
        x_loaded = sem("x_loaded")
        stored = [sem(f"stored{k}") for k in range(2)]
        moved = sem("moved")
        copies_done = sem("copies_done")
        split_done = sem("split_done")
        passed_dve, passed_pool = sem("passed_dve"), sem("passed_pool")
        norm_step, xn_ready, xt_done = sem("norm_step"), sem("xn_ready"), sem("xt_done")
        xh_done, xl_done = sem("xh_done"), sem("xl_done")
        lg_done, route_step, e_done = sem("lg_done"), sem("route_step"), sem("e_done")
        rank_step, rt_done, rt_copied = sem("rank_step"), sem("rt_done"), sem("rt_copied")
        w3_done, w1_done, rwb_done, w2_done = sem("w3_done"), sem("w1_done"), sem("rwb_done"), sem("w2_done")
        u_done, g_done, s_done, p_done = sem("u_done"), sem("g_done"), sem("s_done"), sem("p_done")
        hi_done, lo_done = sem("hi_done"), sem("lo_done")
        ys_done, yt_done, x1_done = sem("ys_done"), sem("yt_done"), sem("x1_done")
        axf_done, axh_done, axl_done = sem("axf_done"), sem("axh_done"), sem("axl_done")
        item_done, item_read = sem("item_done"), sem("item_read")
        kqf_done, kq_hi, kq_lo = sem("kqf_done"), sem("kq_hi"), sem("kq_lo")
        vh_done, vl_done = sem("vh_done"), sem("vl_done")
        a_done, ah_done, al_done, av_done = sem("a_done"), sem("ah_done"), sem("al_done"), sem("av_done")
        og_read, oh_done, o_split = sem("og_read"), sem("oh_done"), sem("o_split")
        z_done, zs_done, zt_done, x2_done = sem("z_done"), sem("zs_done"), sem("zt_done"), sem("x2_done")

        def c(k):
            return col[:, k:k + 1]

        def half(t, h):
            return t[:, h * HALF:(h + 1) * HALF]

        def tile(t, k):
            return t[:, k * P:(k + 1) * P]

        x_dram = x.rearrange("b (p t) d -> b p (t d)", p=P)
        out_dram = out.rearrange("b (p t) d -> b p (t d)", p=P)
        stage = [scratch[:, k * HW:(k + 1) * HW] for k in range(3)]
        acc = [y, tp]
        zbank = [rwb, tp]

        block = ctx.enter_context(nc.Block())

        @block.sync
        def _(sp):
            sp.dma_start(xin[:], x_dram[0]).then_inc(x_loaded, 16)
            sp.dma_start(const[:], consts).then_inc(w_loaded[0], 16)
            sp.dma_start(col[:], cols).then_inc(w_loaded[1], 16)
            sp.dma_start(xb[:, 0:WS], wsmall).then_inc(w_loaded[2], 16)
            sp.dma_start(stage[1], w3).then_inc(w_loaded[3], 16)
            sp.dma_start(stage[0], w1).then_inc(w_loaded[4], 16)
            for h in range(2):
                sp.dma_start(half(res, h)[0:2 * E, :], half(sel, h)).then_inc(stored[h], 16)
            sp.dma_start(xa[0:2 * E, 0:E * H - N], sel[:, N:]).then_inc(w_loaded[6], 16)
            for k in range(3):
                sp.dma_start(b2_f[k * E:(k + 1) * E, :], b2).then_inc(w_loaded[7], 16)
            for k in range(2):
                sp.dma_start(bv_f[k:k + 1, :], bv).then_inc(w_loaded[8], 16)
            sp.dma_start(stage[2], w2).then_inc(w_loaded[5], 16)
            sp.wait_ge(split_done, 6)
            sp.dma_start(b2_h[2 * E:, :].bitcast(F32), b2_lo[2 * E:, :].bitcast(F32)).then_inc(moved, 16)
            sp.dma_start(bv_h[1:2, :].bitcast(F32), bv_lo[1:2, :].bitcast(F32)).then_inc(moved, 16)
            sp.wait_ge(x1_done, 2)
            sp.dma_start(xin[:], x_dram[1]).then_inc(x_loaded, 16)

            def turn(t, batch, following):
                sp.wait_ge(x1_done, (Count(4, 4, t)).value)
                sp.dma_start(xin[:], x_dram[following]).then_inc(x_loaded, 16)
                for h in range(2):
                    sp.wait_ge(x1_done, (Count(5 + h, 4, t)).value)
                    sp.dma_start(half(out_dram[batch], h), half(res, h)).then_inc(stored[h], 16)

            with sp.Fori(0, B - 2) as t:
                turn(t, t, t + 2)
            last = 4 * (B - 2)
            sp.wait_ge(x1_done, last + 4)
            sp.dma_start(xin[:], x_dram[0]).then_inc(x_loaded, 16)
            for h in range(2):
                sp.wait_ge(x1_done, last + 5 + h)
                sp.dma_start(half(out_dram[B - 2], h), half(res, h)).then_inc(stored[h], 16)
            for h in range(2):
                sp.wait_ge(x1_done, 4 * B - 1 + h)
                sp.dma_start(half(out_dram[B - 1], h), half(res, h)).then_inc(stored[h], 16)
            sp.wait_ge(x_loaded, 16 * (B + 1))
            for h in range(2):
                sp.wait_ge(stored[h], 16 * (B + 1))

        @block.tensor
        def _(pe):
            mm = nc.tensor.matmul

            def product(out, a_h, a_l, b_h, b_l, start=True, stop=True):
                mm(out, a_h, b_h, start=start, stop=False)
                mm(out, a_l, b_h, start=False, stop=False)
                return mm(out, a_h, b_l, start=False, stop=stop)

            def turn_x(n):
                pe.wait_ge(xn_ready, (n.u + 1).value)
                if n.before_kind == "ffn":
                    pe.wait_ge(rt_copied, n.before.value)
                elif n.before_kind == "att":
                    pe.wait_ge(axf_done, n.before.value)
                for k in range(TT):
                    last = nc.tensor.transpose(tile(tn, k), tile(xn, k), ident)
                last.then_inc(xt_done, 1)

            def logits(n):
                pe.wait_ge(xl_done, (n.r + 1).value)
                xh, xl = xt_h[n.r.mod(2)], xt_l[n.r.mod(2)]
                for k in range(TT):
                    last = product(tn[:, k * E:(k + 1) * E], tile(xh, k), tile(xl, k),
                                   ws_h[:, O_GW:O_GW + E], ws_l[:, O_GW:O_GW + E])
                last.then_inc(lg_done, 1)

            def turn_route(n):
                pe.wait_ge(route_step, (n.r * ROUTE_STEPS + ROUTE_STEPS).value)
                for k in range(TT):
                    last = nc.tensor.transpose(tile(tn, k), rw3[:, k, :], ident)
                last.then_inc(rt_done, 1)

            def down(ch, j):
                n = ch.q * NBL + j
                rt = rwt[ch.r.mod(2)]
                if j == 0:
                    mm(y[:], b2_h[:], rt[:], start=True, stop=False)
                pe.wait_ge(lo_done, (n + 1).value)
                product(y[:], tile(w2_h, j), tile(w2_l, j), p_h[n.mod(4)][:], p_l[n.mod(4)][:],
                        start=False, stop=(j == NBL - 1)).then_inc(w2_done, 1)

            def turn_y(ch):
                pe.wait_ge(ys_done, (ch.q + 1).value)
                if ch.q.due:
                    pe.wait_ge(x1_done, ch.q.value)
                for k in range(TT):
                    last = nc.tensor.transpose(tile(tp, k), tile(ys, k), ident)
                last.then_inc(yt_done, 1)

            def scores(b, m):
                h, j = divmod(m, KT)
                item = SIM0 + m
                if m in (0, KT // 2, KT):
                    pe.wait_ge(kq_lo, (b * 4 + {0: 2, KT // 2: 3, KT: 4}[m]).value)
                pe.wait_ge(item_read, (b * RING + item - 3).value)
                product(ring[item % 4][:], tile(k_h, j), tile(k_l, j), half(q_h, h), half(q_l, h))\
                    .then_inc(item_done, 1)

            def values(b, m):
                h, j = divmod(m, KT)
                if h == 0 and j % 2 == 0:
                    pe.wait_ge(vl_done, (b * TT + j // 2 + 1).value)
                if m == KT:
                    pe.wait_ge(og_read, (b * 2 + 1).value)
                pe.wait_ge(al_done, (b * (2 * KT) + m + 1).value)
                for k in range(2):
                    cut = slice(j * HID + k * P, j * HID + (k + 1) * P)
                    last = product(acc[k][:], v_h[:, cut], v_l[:, cut], p_h[m % 4][:], p_l[m % 4][:],
                                   start=(j == 0), stop=(j == KT - 1))
                last.then_inc(av_done, 1)

            def project(b, h):
                pe.wait_ge(o_split, (b * 2 + h + 1).value)
                for k in range(2):
                    w = slice(O_OUT + k * D, O_OUT + (k + 1) * D)
                    last = product(zbank[h][:], ws_h[:, w], ws_l[:, w], half(o_h, k), half(o_l, k),
                                   start=(k == 0), stop=(k == 1))
                last.then_inc(z_done, 1)

            def turn_z(b, h):
                pe.wait_ge(zs_done, (b * 2 + h + 1).value)
                for k in range(TT):
                    last = nc.tensor.transpose(tile(zbank[h], k), tile(ys, k), ident)
                last.then_inc(zt_done, 1)

            def ffn(ch, before, pending, preps):
                xh, xl = xt_h[ch.r.mod(2)], xt_l[ch.r.mod(2)]
                att_b = None if before != "att" else ch.att_b
                pe.wait_ge(xl_done, (ch.r + 1).value)
                for j in range(NBL):
                    n = ch.q * NBL + j
                    if j < 2 and before == "att":
                        pe.wait_ge(item_read, (att_b * RING + RING).value)
                    elif j < 2 and before is None:
                        pass
                    else:
                        pe.wait_ge(g_done, (n - 1).value)
                    pair = 2 * n.mod(2)
                    product(ring[pair][:], tile(w3_h, j), tile(w3_l, j), xh[:], xl[:]).then_inc(w3_done, 1)
                    product(ring[pair + 1][:], tile(w1_h, j), tile(w1_l, j), xh[:], xl[:]).then_inc(w1_done, 1)
                    if 1 <= j <= NR:
                        if j == 1:
                            pe.wait_ge(rt_copied, (ch.r + 1).value)
                        if j == 1 and before == "att":
                            pe.wait_ge(x2_done, (att_b * 2 + 1).value)
                        if (ch.q * NR + j - 1).due:
                            pe.wait_ge(p_done, (ch.q * NR + j - 1).value)
                        mm(rwb[:], tile(sel_sb, j - 1), rwt[ch.r.mod(2)][0:2 * E, :],
                           start=True, stop=True).then_inc(rwb_done, 1)
                    if j >= LAG:
                        if j == LAG and before == "ffn":
                            pe.wait_ge(ys_done, ch.q.value)
                        if j == LAG and before == "att":
                            pe.wait_ge(og_read, (att_b * 2 + 2).value)
                        down(ch, j - LAG)
                    elif pending and before == "ffn":
                        down(ch.before, NBL - LAG + j)
                    elif pending and before == "att":
                        values(att_b, 2 * KT - LAG + j)
                    if pending and before == "ffn" and j == 3:
                        turn_y(ch.before)
                    if pending and before == "att" and j == 4:
                        project(att_b, 1)
                    if pending and before == "att" and j == 5:
                        turn_z(att_b, 1)
                    for k, nm in enumerate(preps):
                        if j == (4, 10)[k]:
                            turn_x(nm)
                        if nm.kind == "ffn" and j == 6:
                            logits(nm)
                        if nm.kind == "ffn" and j == 11:
                            turn_route(nm)

            def ffn_rest(ch):
                for j in range(NBL - LAG, NBL):
                    down(ch, j)
                turn_y(ch)

            def attention(b, last_chunk, pending, prep):
                q = last_chunk.q
                for h in range(2):
                    pe.wait_ge(axl_done, (b * 2 + h + 1).value)
                    if h == 0:
                        pe.wait_ge(g_done, (q * NBL + NBL - 1).value)
                    product(ring[h][:], ws_h[:, O_QK:O_QK + D], ws_l[:, O_QK:O_QK + D],
                            half(ax_h, h), half(ax_l, h)).then_inc(item_done, 1)
                if pending:
                    down(last_chunk, NBL - 3)
                pe.wait_ge(g_done, (q * NBL + NBL).value)
                for k in range(TT):
                    item = 2 + k
                    if item >= 4:
                        pe.wait_ge(item_read, (b * RING + item - 3).value)
                    for t in range(2):
                        o = ring[item % 4][:, t * HID:(t + 1) * HID]
                        xs = 2 * k + t
                        mm(o, tile(ax_h, xs), ws_h[:, 0:HID], start=True, stop=False)
                        mm(o, tile(ax_l, xs), ws_h[:, 0:HID], start=False, stop=False)
                        mm(o, tile(ax_h, xs), ws_l[:, 0:HID], start=False, stop=False)
                        last = mm(o, ones[:], bv_h[:], start=False, stop=True)
                    last.then_inc(item_done, 1)
                    if pending and k == 1:
                        down(last_chunk, NBL - 2)
                    if pending and k == 3:
                        down(last_chunk, NBL - 1)
                for k in range(4):
                    item = 2 + TT + k
                    hb, h = divmod(k, 2)
                    pe.wait_ge(item_read, (b * RING + item - 3).value)
                    w = slice(HID + hb * P, HID + (hb + 1) * P)
                    product(ring[item % 4][:], ws_h[:, w], ws_l[:, w], half(ax_h, h), half(ax_l, h))\
                        .then_inc(item_done, 1)
                    if pending and k == 2:
                        turn_y(last_chunk)
                for m in range(2 * KT):
                    scores(b, m)
                    if m == LAG:
                        pe.wait_ge(x1_done, (q + 1).value)
                    if m >= LAG:
                        values(b, m - LAG)
                    if m == 5:
                        turn_x(prep)
                    if m == 8:
                        logits(prep)
                    if m == 12:
                        project(b, 0)
                    if m == 13:
                        turn_z(b, 0)
                    if m == 14:
                        turn_route(prep)

            def attention_rest(b):
                for m in range(2 * KT - LAG, 2 * KT):
                    values(b, m)
                project(b, 1)
                turn_z(b, 1)

            link_chunks_and_run(
                pe, ffn, ffn_rest, attention, attention_rest,
                prepare=lambda n: (turn_x(n), logits(n), turn_route(n)),
                prepare_att=turn_x,
                start=lambda: (pe.wait_ge(w_loaded[0], 16), pe.wait_ge(split_done, SPLITS), pe.wait_ge(moved, 32)),
            )

        @block.scalar
        def _(act):
            act_fn = nc.scalar.activation

            def copy_x(n):
                act.wait_ge(xt_done, (n.u + 1).value)
                if n.kind == "ffn":
                    if (n.q * NBL).due:
                        act.wait_ge(w1_done, (n.q * NBL).value)
                    act_fn(xt_h[n.r.mod(2)][:], tn[:], ACT.Copy).then_inc(xh_done, 1)
                else:
                    if (n.b * 2 + n.half).due:
                        act.wait_ge(axl_done, (n.b * 2 + n.half).value)
                    act_fn(axf[:], tn[:], ACT.Identity, bias=c(C_LNB), scale=c(C_LNS)).then_inc(axf_done, 1)

            def exp(n):
                act.wait_ge(route_step, (n.r * ROUTE_STEPS + 2).value)
                act_fn(ex[:], lg[:], ACT.Exp).then_inc(e_done, 1)

            def copy_route(n):
                act.wait_ge(rt_done, (n.r + 1).value)
                if (n.q * NBL).due:
                    act.wait_ge(w2_done, (n.q * NBL).value)
                act_fn(rwt[n.r.mod(2)][:], tn[0:3 * E, :], ACT.Copy).then_inc(rt_copied, 1)

            def up(ch, j, before):
                n = ch.q * NBL + j
                act.wait_ge(w3_done, (n + 1).value)
                if j < 2 and before == "att":
                    act.wait_ge(a_done, (ch.att_b * (2 * KT) + 2 * KT).value)
                else:
                    if (n - 1).due:
                        act.wait_ge(g_done, (n - 1).value)
                act_fn(u[n.mod(2)][:], ring[2 * n.mod(2)][:], ACT.Identity, bias=c(C_B3 + j))\
                    .then_inc(u_done, 1)

            def silu(ch, j):
                n = ch.q * NBL + j
                act.wait_ge(g_done, (n + 1).value)
                if j < NR:
                    act_fn(g[n.mod(4)][:], g[n.mod(4)][:], ACT.Silu).then_inc(s_done, 1)
                else:
                    act.wait_ge(lo_done, (n - 1).value)
                    act_fn(p[n.mod(2)][:], g[n.mod(4)][:], ACT.Silu).then_inc(s_done, 1)

            def high(ch, j, before=None):
                n = ch.q * NBL + j
                if j < NR:
                    act.wait_ge(p_done, (ch.q * NR + j + 1).value)
                else:
                    act.wait_ge(s_done, (n + 1).value)
                if j < 4 and before == "att":
                    act.wait_ge(av_done, (ch.att_b * (2 * KT) + 2 * KT).value)
                else:
                    if (n - 3).due:
                        act.wait_ge(w2_done, (n - 3).value)
                act_fn(p_h[n.mod(4)][:], p[n.mod(2)][:], ACT.Copy).then_inc(hi_done, 1)

            def half_y(ch):
                act.wait_ge(w2_done, (ch.q * NBL + NBL).value)
                if ch.q.due:
                    act.wait_ge(yt_done, ch.q.value)
                act_fn(ys[:], y[:], ACT.Identity, bias=hb2[:, 0:1], scale=0.5).then_inc(ys_done, 1)

            def ffn(ch, before, pending, preps):
                for j in range(NBL):
                    up(ch, j, before)
                    if j >= 1:
                        silu(ch, j - 1)
                    elif pending and before == "ffn":
                        silu(ch.before, NBL - 1)
                    if j >= 2:
                        high(ch, j - 2, before)
                    elif pending and before == "ffn":
                        high(ch.before, NBL - 2 + j)
                    if pending and before == "ffn" and j == 2:
                        half_y(ch.before)
                    if pending and before == "att" and j == 5:
                        bias_z(ch.att_b, 1)
                    for k, nm in enumerate(preps):
                        if j == (5, 11)[k]:
                            copy_x(nm)
                        if nm.kind == "ffn" and j == 8:
                            exp(nm)
                        if nm.kind == "ffn" and j == NBL - 1:
                            copy_route(nm)

            def ffn_rest(ch):
                silu(ch, NBL - 1)
                high(ch, NBL - 2)
                high(ch, NBL - 1)
                half_y(ch)

            def bias_z(b, h):
                act.wait_ge(z_done, (b * 2 + h + 1).value)
                if h == 0:
                    act.wait_ge(yt_done, (ys_uses_before(b)).value)
                else:
                    act.wait_ge(zt_done, (b * 2 + 1).value)
                act_fn(ys[:], zbank[h][:], ACT.Identity, bias=c(C_BO)).then_inc(zs_done, 1)

            def item(b, k):
                act.wait_ge(item_done, (b * RING + k + 1).value)
                bank = ring[k % 4]
                if k < 2:
                    if (b * 4).due:
                        act.wait_ge(kqf_done, (b * 4).value)
                    act_fn(half(qkf, k), bank[:], ACT.Silu, bias=c(C_BQK)).then_inc(item_read, 1)
                elif k < 2 + TT:
                    if (b * TT + k - 2 - 1).due:
                        act.wait_ge(vl_done, (b * TT + k - 2 - 1).value)
                    act_fn(half(vf, k % 2), bank[:], ACT.Silu).then_inc(item_read, 1)
                else:
                    kk = k - 2 - TT
                    if (b * 2).due:
                        act.wait_ge(og_read, (b * 2).value)
                    act_fn(gate[:, kk * HALF:(kk + 1) * HALF], bank[:], ACT.Silu,
                           bias=c(C_BG + kk // 2)).then_inc(item_read, 1)

            def relu(b, m):
                act.wait_ge(item_done, (b * RING + SIM0 + m + 1).value)
                if m < 2:
                    act.wait_ge(g_done, (after_ffn(b)).value)
                else:
                    act.wait_ge(a_done, (b * (2 * KT) + m - 1).value)
                act_fn(u[m % 2][:], ring[(SIM0 + m) % 4][:], ACT.Relu, scale=1.0 / N).then_inc(item_read, 1)

            def attention(b, last_chunk, pending, prep):
                if pending:
                    silu(last_chunk, NBL - 1)
                    high(last_chunk, NBL - 2)
                item(b, 0)
                item(b, 1)
                if pending:
                    high(last_chunk, NBL - 1)
                for k in range(2, 2 + TT):
                    item(b, k)
                item(b, 2 + TT)
                if pending:
                    half_y(last_chunk)
                for k in range(3 + TT, SIM0):
                    item(b, k)
                for m in range(2 * KT):
                    relu(b, m)
                    if m == 6:
                        copy_x(prep)
                    if m == 10:
                        exp(prep)
                    if m == 13:
                        bias_z(b, 0)
                    if m == 2 * KT - 1:
                        copy_route(prep)

            def start():
                for dst, src, k in ((ws_h[:], xb[:, 0:WS], 2), (w3_h[:], stage[1], 3), (w1_h[:], stage[0], 4),
                                    (w2_h[:], stage[2], 5)):
                    act.wait_ge(w_loaded[k], 16)
                    act_fn(dst, src, ACT.Copy).then_inc(copies_done, 1)
                act.wait_ge(split_done, SPLITS)

            link_chunks_and_run(
                act, ffn, ffn_rest, attention, lambda b: bias_z(b, 1),
                prepare=lambda n: (copy_x(n), exp(n), copy_route(n)),
                prepare_att=copy_x,
                start=start,
            )

        @block.vector
        def _(dve):
            v = nc.vector

            def sources(n):
                return {"xin": xin, "xa": xa, "xb": xb}[n.source]

            def norm(n, part):
                at = n.u * NORM_STEPS
                src = sources(n)
                if part == 0:
                    if at.due:
                        dve.wait_ge(norm_step, at.value)
                    if n.source == "xin" and n.half == 0:
                        dve.wait_ge(x_loaded, ((n.b + 1) * 16).value)
                    if n.source == "xa":
                        dve.wait_ge(x1_done, (n.q_of_source + 1).value)
                    if n.source == "xb":
                        dve.wait_ge(x2_done, (n.b * 2 + n.half + 1).value)
                    for k in range(TT):
                        last = v.bn_stats(st[:, k, :], tile(half(src, n.half), k))
                    last.then_inc(norm_step, 1)
                elif part == 1:
                    if n.u.due:
                        dve.wait_ge(xn_ready, n.u.value)
                    dve.wait_ge(norm_step, (at + 1).value)
                    dve.sem_inc(passed_dve, 1)
                    for k in range(TT):
                        last = v.bn_aggr(mv[:, k, :], st[:, k, :])
                    last.then_inc(norm_step, 1)
                elif part == 2:
                    dve.wait_ge(norm_step, (at + 2).value)
                    one, two = (1.0, EPS) if n.kind == "ffn" else (1.0 + EPS, EPS * EPS)
                    v.tensor_scalar(vv[:], mv[:, :, 1], one, two, ALU.mult, ALU.add).then_inc(norm_step, 1)
                    dve.wait_ge(norm_step, (at + 3).value)
                    v.tensor_scalar(ri[:], vv[:].bitcast(I32), 1, None, ALU.logical_shift_right)\
                        .then_inc(norm_step, 1)
                    dve.wait_ge(norm_step, (at + 4).value)
                    v.tensor_scalar(ri[:], ri[:], -1.0, float(0x5F3759DF), ALU.mult, ALU.add)\
                        .then_inc(norm_step, 1)
                elif part <= 5:
                    k = at + 5 + 3 * (part - 3)
                    r = ri[:].bitcast(F32)
                    dve.wait_ge(norm_step, k.value)
                    v.scalar_tensor_tensor(t1[:], r, -0.5, r, ALU.mult, ALU.mult).then_inc(norm_step, 1)
                    dve.wait_ge(norm_step, (k + 1).value)
                    v.tensor_tensor(t2[:], t1[:], vv[:], ALU.mult).then_inc(norm_step, 1)
                    dve.wait_ge(norm_step, (k + 2).value)
                    v.scalar_tensor_tensor(r, t2[:], 1.5, r, ALU.add, ALU.mult).then_inc(norm_step, 1)
                else:
                    dve.wait_ge(norm_step, (at + NORM_STEPS).value)
                    if n.u.due:
                        dve.wait_ge(xt_done, n.u.value)
                    for k in range(TT):
                        last = v.tensor_scalar(tile(xn, k), tile(half(src, n.half), k), mv[:, k, 0:1],
                                               ri[:, k:k + 1].bitcast(F32), ALU.subtract, ALU.mult)
                    last.then_inc(xn_ready, 1)

            def low_x(n):
                dve.wait_ge(xh_done, (n.r + 1).value)
                k = n.r.mod(2)
                v.tensor_tensor(xt_l[k][:], tn[:], xt_h[k][:].bitcast(F32), ALU.subtract).then_inc(xl_done, 1)

            def high_ax(n):
                dve.wait_ge(axf_done, (n.b * 2 + n.half + 1).value)
                v.tensor_copy(half(ax_h, n.half), axf[:]).then_inc(axh_done, 1)

            def wide(t):
                return t[:].unsqueeze(2).to_broadcast([P, TT, E])

            def route(n, part):
                at = n.r * ROUTE_STEPS
                if part == 0:
                    l3 = tn[:, 0:TT * E].rearrange("p (t e) -> p t e", e=E)
                    if at.due:
                        dve.wait_ge(route_step, at.value)
                    dve.wait_ge(lg_done, (n.r + 1).value)
                    v.tensor_reduce(mx[:], l3, AX.X, ALU.max).then_inc(route_step, 1)
                    dve.wait_ge(route_step, (at + 1).value)
                    v.tensor_tensor(lg[:], l3, wide(mx), ALU.subtract).then_inc(route_step, 1)
                elif part == 1:
                    dve.wait_ge(e_done, (n.r + 1).value)
                    v.tensor_reduce(sm[:], ex[:], AX.X, ALU.add).then_inc(route_step, 1)
                    dve.wait_ge(route_step, (at + 3).value)
                    v.reciprocal(rc[:], sm[:]).then_inc(route_step, 1)
                elif part == 2:
                    dve.wait_ge(route_step, (at + 4).value)
                    v.tensor_tensor(sc[:], ex[:], wide(rc), ALU.mult).then_inc(route_step, 1)
                    dve.wait_ge(route_step, (at + 5).value)
                    gb = col[:, C_GB:C_GB + E].unsqueeze(1).to_broadcast([P, TT, E])
                    v.tensor_tensor(bi[:], sc[:], gb, ALU.add).then_inc(route_step, 1)
                elif part == 3:
                    dve.wait_ge(rank_step, (n.r * RANK_STEPS + RANK_STEPS).value)
                    v.tensor_reduce(rank[:], gt[:].rearrange("p t (e f) -> p t e f", f=E), AX.X, ALU.add)\
                        .then_inc(route_step, 1)
                    dve.wait_ge(route_step, (at + 7).value)
                    v.scalar_tensor_tensor(rw[:], rank[:], 2.0, sc[:], ALU.is_lt, ALU.mult).then_inc(route_step, 1)
                    dve.wait_ge(route_step, (at + 8).value)
                    v.tensor_copy(rwh[:], rw[:]).then_inc(route_step, 1)
                else:
                    dve.wait_ge(route_step, (at + 9).value)
                    if n.r.due:
                        dve.wait_ge(rt_done, n.r.value)
                    for k in (0, 2):
                        last = v.tensor_copy(rw3[:, :, k * E:(k + 1) * E], rwh[:].bitcast(F32))
                    last.then_inc(route_step, 1)
                    v.tensor_tensor(rw3[:, :, E:2 * E], rw[:], rwh[:].bitcast(F32), ALU.subtract)\
                        .then_inc(route_step, 1)

            def product(ch, j, before):
                n = ch.q * NBL + j
                dve.wait_ge(w1_done, (n + 1).value)
                dve.wait_ge(u_done, (n + 1).value)
                if j < 4 and before == "att":
                    dve.wait_ge(al_done, (ch.att_b * (2 * KT) + 2 * KT).value)
                else:
                    if (n - 3).due:
                        dve.wait_ge(s_done, (n - 3).value)
                    done = ch.q * NR + max(j - 3, 0)
                    if done.due:
                        dve.wait_ge(p_done, done.value)
                v.scalar_tensor_tensor(g[n.mod(4)][:], ring[2 * n.mod(2) + 1][:], c(C_B1 + j), u[n.mod(2)][:],
                                       ALU.add, ALU.mult).then_inc(g_done, 1)

            def weigh(ch, j):
                n = ch.q * NBL + j
                dve.wait_ge(s_done, (n + 1).value)
                dve.wait_ge(rwb_done, (ch.q * NR + j + 1).value)
                if (n - 1).due:
                    dve.wait_ge(lo_done, (n - 1).value)
                v.tensor_tensor(p[n.mod(2)][:], g[n.mod(4)][:], rwb[:], ALU.mult).then_inc(p_done, 1)

            def residual(ch):
                dve.wait_ge(yt_done, (ch.q + 1).value)
                src, dst = (xin, xa) if ch.ffn == 1 else (xb, res)
                if ch.ffn == 2:
                    dve.wait_ge(stored[ch.half], (ch.b * 16 + 16).value)
                else:
                    if (ch.b * 2 + ch.half - 1).due:
                        dve.wait_ge(x2_done, (ch.b * 2 + ch.half - 1).value)
                v.tensor_tensor(half(dst, ch.half), half(src, ch.half), tp[:], ALU.add).then_inc(x1_done, 1)

            def gate_o(b, h):
                dve.wait_ge(av_done, (b * (2 * KT) + (h + 1) * KT).value)
                dve.wait_ge(item_read, (b * RING + SIM0).value)
                if (b * 2 + h).due:
                    dve.wait_ge(o_split, (b * 2 + h).value)
                for k in range(2):
                    last = v.tensor_tensor(half(o_f, k), acc[k][:],
                                           gate[:, (2 * k + h) * HALF:(2 * k + h + 1) * HALF], ALU.mult)
                last.then_inc(og_read, 1)

            def split_o(b, h, part):
                if part == 0:
                    dve.wait_ge(og_read, (b * 2 + h + 1).value)
                    if (b * 2 + h).due:
                        dve.wait_ge(z_done, (b * 2 + h).value)
                    v.tensor_copy(o_h[:], o_f[:]).then_inc(oh_done, 1)
                else:
                    dve.wait_ge(oh_done, (b * 2 + h + 1).value)
                    v.tensor_tensor(o_l[:], o_f[:], o_h[:].bitcast(F32), ALU.subtract).then_inc(o_split, 1)

            def residual_z(b, h):
                dve.wait_ge(zt_done, (b * 2 + h + 1).value)
                dve.wait_ge(x1_done, (b * 4 + h + 1).value)
                v.tensor_tensor(half(xb, h), half(xa, h), zbank[h][:], ALU.add).then_inc(x2_done, 1)

            def ffn(ch, before, pending, preps):
                for j in range(NBL):
                    product(ch, j, before)
                    slot(ch, 2 * j, before, pending, preps)
                    if 1 <= j <= NR:
                        weigh(ch, j - 1)
                    slot(ch, 2 * j + 1, before, pending, preps)

            def slot(ch, s, before, pending, preps):
                if pending and before == "ffn" and s == 8:
                    residual(ch.before)
                if pending and before == "att":
                    if s == 5:
                        gate_o(ch.att_b, 1)
                    if s == 6:
                        split_o(ch.att_b, 1, 0)
                    if s == 7:
                        split_o(ch.att_b, 1, 1)
                    if s == 12:
                        residual_z(ch.att_b, 1)
                for k, nm in enumerate(preps):
                    first = (0, 13)[k]
                    if first <= s < first + 7:
                        norm(nm, s - first)
                    if nm.kind == "att" and s == first + 10:
                        high_ax(nm)
                    if nm.kind == "ffn":
                        if s == 11:
                            low_x(nm)
                        if s == 14:
                            route(nm, 0)
                        if s in (17, 18):
                            route(nm, s - 16)
                        if s in (21, 22):
                            route(nm, s - 18)

            def kq(b, k):
                dve.wait_ge(item_read, (b * RING + k // 2 + 1).value)
                if (b * 4 + k - 1).due:
                    dve.wait_ge(kq_lo, (b * 4 + k - 1).value)
                w, bb = (C_KW, C_KB) if k % 2 == 0 else (C_QW, C_QB)
                v.tensor_scalar(half(kqt, k % 2), half(qkf, k // 2), c(w), c(bb), ALU.mult, ALU.add)\
                    .then_inc(kqf_done, 1)
                dve.wait_ge(kqf_done, (b * 4 + k + 1).value)
                v.tensor_copy(half((k_h, q_h)[k % 2], k // 2), half(kqt, k % 2)).then_inc(kq_hi, 1)

            def high_v(b, k):
                dve.wait_ge(item_read, (b * RING + 2 + k + 1).value)
                v.tensor_copy(v_h[:, k * HALF:(k + 1) * HALF], half(vf, k % 2)).then_inc(vh_done, 1)

            def square(b, m):
                dve.wait_ge(item_read, (b * RING + SIM0 + m + 1).value)
                if m == 0:
                    dve.wait_ge(s_done, (after_ffn(b)).value)
                    dve.wait_ge(w2_done, (after_ffn(b)).value)
                    dve.wait_ge(p_done, (b * (4 * NR) + 2 * NR).value)
                if m >= 4:
                    dve.wait_ge(al_done, (b * (2 * KT) + m - 3).value)
                v.tensor_tensor(g[m % 4][:], u[m % 2][:], u[m % 2][:], ALU.mult).then_inc(a_done, 1)
                dve.wait_ge(a_done, (b * (2 * KT) + m + 1).value)
                if m >= 4:
                    dve.wait_ge(av_done, (b * (2 * KT) + m - 3).value)
                v.tensor_copy(p_h[m % 4][:], g[m % 4][:]).then_inc(ah_done, 1)

            def attention(b, last_chunk, pending, prep):
                kq(b, 0)
                kq(b, 1)
                high_v(b, 0)
                high_v(b, 1)
                kq(b, 2)
                high_v(b, 2)
                kq(b, 3)
                high_v(b, 3)
                if pending:
                    residual(last_chunk)
                for m in range(2 * KT):
                    square(b, m)
                    if m < 5:
                        norm(prep, m)
                    if m == 5:
                        norm(prep, 5)
                    if m == 5:
                        norm(prep, 6)
                    if m == 7:
                        low_x(prep)
                    if m == 9:
                        route(prep, 0)
                    if m == 10:
                        gate_o(b, 0)
                    if m == 11:
                        split_o(b, 0, 0)
                        split_o(b, 0, 1)
                    if m in (12, 13):
                        route(prep, m - 11)
                    if m == 14:
                        residual_z(b, 0)
                        route(prep, 3)
                        route(prep, 4)

            def attention_rest(b):
                gate_o(b, 1)
                split_o(b, 1, 0)
                split_o(b, 1, 1)
                residual_z(b, 1)

            def prepare(n):
                for k in range(7):
                    norm(n, k)
                low_x(n)
                for k in range(5):
                    route(n, k)

            def prepare_att(n):
                for k in range(7):
                    norm(n, k)
                high_ax(n)

            def start():
                dve.wait_ge(w_loaded[1], 16)
                v.tensor_scalar(hb2[:], c(C_SB2), 0.5, None, ALU.mult).then_inc(split_done, 1)
                v.memset(rw3[:], 0.0).then_inc(split_done, 1)
                dve.wait_ge(w_loaded[0], 16)
                v.tensor_copy(ones[:], ones_f).then_inc(split_done, 1)
                dve.wait_ge(w_loaded[7], 48)
                dve.wait_ge(w_loaded[8], 32)
                v.tensor_copy(b2_h[:], b2_f[:])
                v.tensor_copy(bv_h[:], bv_f[:]).then_inc(split_done, 1)
                dve.wait_ge(split_done, 4)
                v.tensor_tensor(b2_lo[:], b2_f[:], b2_h[:].bitcast(F32), ALU.subtract).then_inc(split_done, 1)
                v.tensor_tensor(bv_lo[:], bv_f[:], bv_h[:].bitcast(F32), ALU.subtract).then_inc(split_done, 1)
                dve.wait_ge(w_loaded[6], 16)
                dve.wait_ge(stored[0], 16)
                dve.wait_ge(stored[1], 16)
                v.tensor_copy(sel_sb[:, 0:N], res[0:2 * E, 0:N])
                v.tensor_copy(sel_sb[:, N:], xa[0:2 * E, 0:E * H - N]).then_inc(split_done, 1)
                for k, (dst, src, hi) in enumerate(((ws_l[:], xb[:, 0:WS], ws_h), (w3_l[:], stage[1], w3_h),
                                                    (w1_l[:], stage[0], w1_h), (w2_l[:], stage[2], w2_h))):
                    dve.wait_ge(copies_done, k + 1)
                    v.tensor_tensor(dst, src, hi[:].bitcast(F32), ALU.subtract).then_inc(split_done, 1)

            link_chunks_and_run(dve, ffn, residual, attention, attention_rest,
                                prepare=prepare, prepare_att=prepare_att, start=start)

        @block.gpsimd
        def _(pool):
            gp = nc.gpsimd

            def low(ch, j):
                n = ch.q * NBL + j
                pool.wait_ge(hi_done, (n + 1).value)
                gp.tensor_tensor(p_l[n.mod(4)][:], p[n.mod(2)][:], p_h[n.mod(4)][:].bitcast(F32),
                                 ALU.subtract).then_inc(lo_done, 1)

            def rank_experts(n):
                at = n.r * RANK_STEPS
                mine = bi[:].unsqueeze(3).to_broadcast([P, TT, E, E])
                other = bi[:].unsqueeze(2).to_broadcast([P, TT, E, E])
                d4 = diff[:].rearrange("p t (e f) -> p t e f", f=E)
                pool.wait_ge(route_step, (n.r * ROUTE_STEPS + 6).value)
                gp.tensor_tensor(d4, other, mine, ALU.subtract).then_inc(rank_step, 1)
                pool.wait_ge(rank_step, (at + 1).value)
                pool.sem_inc(passed_pool, 1)
                gp.tensor_scalar(gt[:], diff[:], 0.0, None, ALU.is_gt).then_inc(rank_step, 1)
                gp.tensor_scalar(eq[:], diff[:], 0.0, None, ALU.is_equal).then_inc(rank_step, 1)
                pool.wait_ge(rank_step, (at + 3).value)
                gp.tensor_tensor(eq[:], eq[:], before.unsqueeze(1).to_broadcast([P, TT, E * E]), ALU.mult)\
                    .then_inc(rank_step, 1)
                pool.wait_ge(rank_step, (at + 4).value)
                gp.tensor_tensor(gt[:], gt[:], eq[:], ALU.add).then_inc(rank_step, 1)

            def low_ax(n):
                pool.wait_ge(axh_done, (n.b * 2 + n.half + 1).value)
                gp.tensor_tensor(half(ax_l, n.half), axf[:], half(ax_h, n.half).bitcast(F32), ALU.subtract)\
                    .then_inc(axl_done, 1)

            def ffn(ch, before, pending, preps):
                for j in range(NBL):
                    if j >= 2:
                        low(ch, j - 2)
                    elif pending and before == "ffn":
                        low(ch.before, NBL - 2 + j)
                    for k, nm in enumerate(preps):
                        if nm.kind == "ffn" and j == 9:
                            rank_experts(nm)
                        if nm.kind == "att" and j == (6, 12)[k]:
                            low_ax(nm)

            def ffn_rest(ch):
                low(ch, NBL - 2)
                low(ch, NBL - 1)

            def low_kq(b, k):
                pool.wait_ge(kq_hi, (b * 4 + k + 1).value)
                hi, lo = ((k_h, k_l), (q_h, q_l))[k % 2]
                gp.tensor_tensor(half(lo, k // 2), half(kqt, k % 2), half(hi, k // 2).bitcast(F32),
                                 ALU.subtract).then_inc(kq_lo, 1)

            def low_v(b, k):
                pool.wait_ge(vh_done, (b * TT + k + 1).value)
                cut = slice(k * HALF, (k + 1) * HALF)
                gp.tensor_tensor(v_l[:, cut], half(vf, k % 2), v_h[:, cut].bitcast(F32), ALU.subtract)\
                    .then_inc(vl_done, 1)

            def low_a(b, m):
                pool.wait_ge(ah_done, (b * (2 * KT) + m + 1).value)
                gp.tensor_tensor(p_l[m % 4][:], g[m % 4][:], p_h[m % 4][:].bitcast(F32), ALU.subtract)\
                    .then_inc(al_done, 1)

            def attention(b, last_chunk, pending, prep):
                if pending:
                    low(last_chunk, NBL - 2)
                low_kq(b, 0)
                if pending:
                    low(last_chunk, NBL - 1)
                low_kq(b, 1)
                low_v(b, 0)
                low_v(b, 1)
                low_kq(b, 2)
                low_v(b, 2)
                low_kq(b, 3)
                low_v(b, 3)
                for m in range(2 * KT):
                    low_a(b, m)
                    if m == 13:
                        rank_experts(prep)

            link_chunks_and_run(pool, ffn, ffn_rest, attention, None,
                                prepare=rank_experts, prepare_att=low_ax,
                                start=lambda: pool.wait_ge(w_loaded[0], 16))


SPLITS = 11


def after_ffn(b):
    return b * (4 * NBL) + 2 * NBL


def ys_uses_before(b):
    return b * 4 + 2


def link_chunks_and_run(eng, ffn, ffn_rest, attention, attention_rest, prepare, prepare_att, start):
    def follow(n, before_kind, before):
        n.before_kind, n.before = before_kind, before
        return n

    start()
    c, first, second, att, following = phases_before()
    c[1].before = c[0]
    follow(first, None, None)
    follow(second, "ffn", Count(1))
    follow(att[0], "ffn", Count(2))
    follow(att[1], "att", Count(1))
    follow(following, "att", Count(2))
    for h in range(2):
        att[h].q_of_source = Count(h)
    prepare(first)
    ffn(c[0], None, False, [second])
    ffn(c[1], "ffn", True, [])
    ffn_rest(c[1])
    for n in att:
        prepare_att(n)
    attention(Count(0), c[1], False, following)

    with eng.Fori(0, B - 1) as turn:
        c, preps, b, following = phases_of_turn(turn)
        for k in range(1, 4):
            c[k].before = c[k - 1]
        c[0].att_b = b - 1
        follow(preps[0][0], "ffn", c[0].r + 1)
        follow(preps[1][0], "ffn", c[1].r + 1)
        follow(preps[2][0], "ffn", c[2].r + 1)
        follow(preps[3][0], "ffn", c[3].r + 1)
        follow(preps[3][1], "att", b * 2 + 1)
        follow(following, "att", b * 2 + 2)
        for h in range(2):
            preps[3][h].q_of_source = c[h].q
        ffn(c[0], "att", True, preps[0])
        for k in range(1, 4):
            ffn(c[k], "ffn", True, preps[k])
        attention(b, c[3], True, following)

    c, first, second = phases_after()
    c[0].att_b = Count(B - 1)
    c[1].before = c[0]
    follow(first, "ffn", Count(4 * B - 1))
    follow(second, "ffn", Count(4 * B))
    if attention_rest is not None:
        attention_rest(Count(B - 1))
    prepare(first)
    ffn(c[0], "att", False, [second])
    ffn(c[1], "ffn", True, [])
    ffn_rest(c[1])


def kernel(L0_attn_x, L0_attn_ln_scale, L0_attn_ln_bias, L0_attn_W_hidden, L0_attn_b_hidden, L0_attn_W_qk,
           L0_attn_b_qk, L0_attn_os_weight, L0_attn_os_bias, L0_attn_W_out, L0_attn_b_out, L0_ffn_gate_w,
           L0_ffn_gate_b, L0_ffn_w1, L0_ffn_b1, L0_ffn_w3, L0_ffn_b3, L0_ffn_w2, L0_ffn_b2, L0_ffn_sw1,
           L0_ffn_sb1, L0_ffn_sw3, L0_ffn_sb3, L0_ffn_sw2, L0_ffn_sb2):
    import concourse.bacc as bacc
    from concourse.bass_utils import run_bass_kernel_spmd

    def arr(a):
        return np.ascontiguousarray(a)

    def blocks(flat):
        pad = np.zeros((HW - flat.shape[-1],), flat.dtype) if flat.ndim == 1 else \
            np.zeros((flat.shape[0], HW - flat.shape[-1]), flat.dtype)
        return np.concatenate([flat, pad], axis=-1)

    def wide(w, sw):
        w = arr(w)
        return blocks(np.concatenate([w.transpose(1, 0, 2).reshape(D, E * H), arr(sw)], axis=1))

    def by_block(b, sb):
        return blocks(np.concatenate([arr(b).reshape(-1), arr(sb)])).reshape(NBL, P).T

    down = np.concatenate([arr(L0_ffn_w2).reshape(E * H, D), arr(L0_ffn_sw2)], axis=0)
    down = blocks(arr(down.T)).T.reshape(NBL, P, D).transpose(1, 0, 2).reshape(P, HW)
    osw, osb, bh = arr(L0_attn_os_weight), arr(L0_attn_os_bias), arr(L0_attn_b_hidden)
    one_cols = [L0_ffn_sb2, L0_attn_ln_scale, L0_attn_ln_bias, L0_attn_b_qk, bh[HID:HID + P], bh[HID + P:],
                osw[0], osw[1], osb[0], osb[1], L0_attn_b_out]
    cols = np.concatenate([by_block(L0_ffn_b1, L0_ffn_sb1), by_block(L0_ffn_b3, L0_ffn_sb3)]
                          + [arr(a).reshape(P, 1) for a in one_cols]
                          + [np.repeat(arr(L0_ffn_gate_b).reshape(1, E), P, axis=0)], axis=1)
    before = np.tril(np.ones((E, E), np.float32), -1).reshape(1, E * E)
    consts = np.concatenate([np.eye(P, dtype=np.float32), np.repeat(before, P, axis=0),
                             np.ones((P, P), np.float32)], axis=1)
    sel = np.repeat(np.tile(np.eye(E, dtype=np.float32), (2, 1)), H, axis=1)
    wo = arr(L0_attn_W_out).reshape(2, P, D).transpose(1, 0, 2).reshape(P, 2 * D)
    wsmall = np.concatenate([arr(L0_attn_W_hidden), arr(L0_attn_W_qk), wo, arr(L0_ffn_gate_w).T], axis=1)
    arrays = {
        "x": arr(L0_attn_x), "cols": arr(cols), "consts": arr(consts), "sel": arr(sel),
        "w1": arr(wide(L0_ffn_w1, L0_ffn_sw1)), "w3": arr(wide(L0_ffn_w3, L0_ffn_sw3)), "w2": arr(down),
        "wsmall": arr(wsmall), "b2": arr(L0_ffn_b2), "bv": arr(bh[:HID].reshape(1, HID)),
    }
    nc = bacc.Bacc("TRN2", target_bir_lowering=False, num_devices=1)
    args = [nc.dram_tensor(k, a.shape, mybir.dt.from_np(a.dtype), kind="ExternalInput").ap()
            for k, a in arrays.items()]
    out = nc.dram_tensor("out", (B, N, D), F32, kind="ExternalOutput").ap()
    build(nc, *args, out)
    got = run_bass_kernel_spmd(nc, [arrays], core_ids=[0])
    return got.results[0]["out"]
```

```python
from contextlib import ExitStack

import numpy as np

import concourse.bass as bass
from concourse import mybir

F32 = mybir.dt.float32
F32R = mybir.dt.float32r
I32 = mybir.dt.int32
ALU = mybir.AluOpType
ACT = mybir.ActivationFunctionType
AX = mybir.AxisListType

B, N, D = 8, 1024, 128
E, H, HID = 8, 176, 256
P = 128
HALF = N // 2
TT = HALF // P
NR = E * H // P
NBL = -(-(E + 1) * H // P)
HW = NBL * P
KT = N // P
RING = 2 + TT + 4 + 2 * KT
SIM0 = 2 + TT
LAG = 3
NORM_STEPS, ROUTE_STEPS, TABLE_STEPS = 14, 13, 4
EPS = 1e-5
TINY = 2.0 ** -120

C_B1, C_B3 = 0, NBL
C_SB2 = 2 * NBL
C_LNS, C_LNB, C_BQK, C_BG = C_SB2 + 1, C_SB2 + 2, C_SB2 + 3, C_SB2 + 4
C_QW, C_KW, C_QB, C_KB = C_BG + 2, C_BG + 3, C_BG + 4, C_BG + 5
C_BO = C_BG + 6
C_GB = C_BO + 1
NCOL = C_GB + E


class Count:

    def __init__(self, first, step=0, turn=None):
        self.first, self.step, self.turn = first, step, turn

    def __add__(self, k):
        return Count(self.first + k, self.step, self.turn)

    def __sub__(self, k):
        return self + -k

    def __mul__(self, k):
        return Count(self.first * k, self.step * k, self.turn)

    @property
    def due(self):
        return self.turn is not None or self.first > 0

    @property
    def value(self):
        assert self.first > 0
        return self.first if self.turn is None else self.turn * self.step + self.first

    def mod(self, m):
        assert self.step % m == 0
        return self.first % m


class Chunk:

    def __init__(self, q, r, b, half, ffn):
        self.q, self.r, self.b, self.half, self.ffn = q, r, b, half, ffn


class Norm:

    def __init__(self, u, i, kind, source, b, half, r=None, q=None):
        self.u, self.i, self.kind, self.source, self.b, self.half, self.r, self.q = u, i, kind, source, b, half, r, q
        self.table = r
        self.after_att = False
        self.halves = (half,) if kind == "ffn" else (0, 1)


def score_item(m):
    return SIM0 + m + min(m, 4)


def gate_item(k):
    return SIM0 + 2 * k + 1


def bank_of(item):
    return (item if item < SIM0 else item + 2) % 4


def read_before(item):
    return item - 3 if item < SIM0 or item >= SIM0 + 2 else item - 1


def phases_before():
    c = [Chunk(Count(k), Count(k), Count(0), k, 1) for k in range(2)]
    first = Norm(Count(0), Count(0), "ffn", "xin", Count(0), 0, Count(0), Count(-1))
    second = Norm(Count(1), Count(1), "ffn", "xin", Count(0), 1, Count(1), Count(0))
    att = Norm(Count(2), Count(2), "att", "xa", Count(0), 0)
    following = Norm(Count(3), Count(4), "ffn", "xin", Count(1), 0, Count(2), Count(1))
    return c, first, second, att, following


def phases_of_turn(turn):
    q, u, i = Count(2, 4, turn), Count(4, 5, turn), Count(5, 6, turn)
    b, last = Count(1, 1, turn), Count(0, 1, turn)
    c = [Chunk(q + k, q + k, b if k < 2 else last, k % 2, 1 if k < 2 else 2) for k in range(4)]
    preps = [
        Norm(u, i, "ffn", "xin", b, 1, q + 1, q),
        Norm(u + 1, i + 1, "ffn", "xb", last, 0, q + 2, q + 1),
        Norm(u + 2, i + 2, "ffn", "xb", last, 1, q + 3, q + 2),
        Norm(u + 3, i + 3, "att", "xa", b, 0),
    ]
    following = Norm(u + 4, i + 5, "ffn", "xin", b + 1, 0, q + 4, q + 3)
    return c, preps, b, following


def phases_after():
    q, u, i, b = 4 * B - 2, 5 * B - 1, 6 * B - 1, Count(B - 1)
    c = [Chunk(Count(q + k), Count(q + 1 + k), b, k, 2) for k in range(2)]
    first = Norm(Count(u), Count(i), "ffn", "xb", b, 0, Count(q + 1), Count(q))
    second = Norm(Count(u + 1), Count(i + 1), "ffn", "xb", b, 1, Count(q + 2), Count(q))
    first.table, second.table = c[0].q, c[1].q
    return c, first, second


def build(nc, x, cols, consts, sel, w1, w3, w2, wsmall, b2, bv, out):
    with ExitStack() as ctx:
        def sb(name, shape, dt=F32):
            return ctx.enter_context(nc.sbuf_tensor(name, shape, dt))

        def sem(name):
            return ctx.enter_context(nc.semaphore(name))

        ring = [ctx.enter_context(nc.psum_tensor(f"ring{k}", [P, HALF], F32)) for k in range(4)]
        rwb = ctx.enter_context(nc.psum_tensor("rwb", [P, HALF], F32))
        y = ctx.enter_context(nc.psum_tensor("y", [P, HALF], F32))
        tn = ctx.enter_context(nc.psum_tensor("tn", [P, HALF], F32))
        tp = ctx.enter_context(nc.psum_tensor("tp", [P, HALF], F32))

        w1_h, w1_l = sb("w1_h", [P, HW], F32R), sb("w1_l", [P, HW], F32R)
        w3_h, w3_l = sb("w3_h", [P, HW], F32R), sb("w3_l", [P, HW], F32R)
        w2_h, w2_l = sb("w2_h", [P, HW], F32R), sb("w2_l", [P, HW], F32R)
        WS = 2 * HID + D + 2 * D + E
        ws_h, ws_l = sb("ws_h", [P, WS], F32R), sb("ws_l", [P, WS], F32R)
        O_QK, O_OUT, O_GW = 2 * HID, 2 * HID + D, 2 * HID + 3 * D
        sel_sb = sb("sel_sb", [2 * E, E * H], F32R)
        b2_f = sb("b2_f", [3 * E, D])
        b2_h, b2_lo = sb("b2_h", [3 * E, D], F32R), sb("b2_lo", [3 * E, D], F32R)
        bv_f = sb("bv_f", [2, HID])
        bv_h, bv_lo = sb("bv_h", [2, HID], F32R), sb("bv_lo", [2, HID], F32R)
        ones = sb("ones", [2, P], F32R)
        col = sb("col", [P, NCOL])
        hb2 = sb("hb2", [P, 1])
        const = sb("const", [P, P + E * E + P])
        ident, before = const[:, 0:P], const[:, P:P + E * E]
        ones_f = const[0:2, P + E * E:]

        xin, xa, xb = sb("xin", [P, KT * D]), sb("xa", [P, KT * D]), sb("xb", [P, KT * D])
        res = sb("res", [P, KT * D])
        st, mv = sb("st", [P, KT, 6]), sb("mv", [P, KT, 2])
        vv, ri, t1, t2 = sb("vv", [P, KT]), sb("ri", [P, KT], I32), sb("t1", [P, KT]), sb("t2", [P, KT])
        xn = sb("xn", [P, HALF])
        xt_h = [sb(f"xt_h{k}", [P, HALF], F32R) for k in range(2)]
        xt_l = [sb(f"xt_l{k}", [P, HALF], F32R) for k in range(2)]
        mx, sm, rc = sb("mx", [P, TT]), sb("sm", [P, TT]), sb("rc", [P, TT])
        lg, sl, dn, ex, sc, bi = (sb(k, [P, TT, E]) for k in ("lg", "sl", "dn", "ex", "sc", "bi"))
        diff = sb("diff", [P, TT, E * E])
        gt, eq = sb("gt", [P, TT, E * E]), sb("eq", [P, TT, E * E])
        rank, rw = sb("rank", [P, TT, E]), sb("rw", [P, TT, E])
        rwh = sb("rwh", [P, TT, E], F32R)
        rw3 = sb("rw3", [P, TT, P])
        rwt = [sb(f"rwt{k}", [3 * E, HALF], F32R) for k in range(2)]
        u = [sb(f"u{k}", [P, HALF]) for k in range(2)]
        g = [sb(f"g{k}", [P, HALF]) for k in range(4)]
        p = [sb(f"p{k}", [P, HALF]) for k in range(2)]
        p_h = [sb(f"p_h{k}", [P, HALF], F32R) for k in range(4)]
        p_l = [sb(f"p_l{k}", [P, HALF], F32R) for k in range(4)]
        ys = sb("ys", [P, HALF])
        axf = sb("axf", [P, HALF])
        ax_h, ax_l = sb("ax_h", [P, N], F32R), sb("ax_l", [P, N], F32R)
        scratch = sb("scratch", [P, 5 * N])
        qkf, kqt = scratch[:, 0:N], scratch[:, N:2 * N]
        vf, gate = scratch[:, 2 * N:3 * N], scratch[:, 3 * N:5 * N]
        k_h, k_l = sb("k_h", [P, N], F32R), sb("k_l", [P, N], F32R)
        q_h, q_l = sb("q_h", [P, N], F32R), sb("q_l", [P, N], F32R)
        v_h, v_l = sb("v_h", [P, KT * HID], F32R), sb("v_l", [P, KT * HID], F32R)
        o_f, o_h, o_l = sb("o_f", [P, N]), sb("o_h", [P, N], F32R), sb("o_l", [P, N], F32R)

        w_loaded = [sem(f"w_loaded{k}") for k in range(9)]
        x_loaded = sem("x_loaded")
        stored = [sem(f"stored{k}") for k in range(2)]
        moved = sem("moved")
        copies_done = sem("copies_done")
        split_done = sem("split_done")
        passed_dve = sem("passed_dve")
        table_step = sem("table_step")
        norm_step, xn_ready, xt_done = sem("norm_step"), sem("xn_ready"), sem("xt_done")
        xh_done, xl_done = sem("xh_done"), sem("xl_done")
        lg_done, route_step, sl_done = sem("lg_done"), sem("route_step"), sem("sl_done")
        rt_done, rt_copied = sem("rt_done"), sem("rt_copied")
        w3_done, w1_done, rwb_done, w2_done = sem("w3_done"), sem("w1_done"), sem("rwb_done"), sem("w2_done")
        u_done, g_done, s_done, p_done = sem("u_done"), sem("g_done"), sem("s_done"), sem("p_done")
        hi_done, lo_done = sem("hi_done"), sem("lo_done")
        ys_done, yt_done, x1_done = sem("ys_done"), sem("yt_done"), sem("x1_done")
        axf_done, axh_done, axl_done = sem("axf_done"), sem("axh_done"), sem("axl_done")
        item_done, item_read = sem("item_done"), sem("item_read")
        kqf_done, kq_hi, kq_lo = sem("kqf_done"), sem("kq_hi"), sem("kq_lo")
        vh_done, vl_done = sem("vh_done"), sem("vl_done")
        a_done, ah_done, al_done, av_done = sem("a_done"), sem("ah_done"), sem("al_done"), sem("av_done")
        og_read, oh_done, o_split = sem("og_read"), sem("oh_done"), sem("o_split")
        z_done, zs_done, zt_done, x2_done = sem("z_done"), sem("zs_done"), sem("zt_done"), sem("x2_done")

        def c(k):
            return col[:, k:k + 1]

        def half(t, h):
            return t[:, h * HALF:(h + 1) * HALF]

        def tile(t, k):
            return t[:, k * P:(k + 1) * P]

        x_dram = x.rearrange("b (p t) d -> b p (t d)", p=P)
        out_dram = out.rearrange("b (p t) d -> b p (t d)", p=P)
        stage = [scratch[:, k * HW:(k + 1) * HW] for k in range(3)]
        acc = [y, tp]
        zbank = [rwb, tp]

        block = ctx.enter_context(nc.Block())

        @block.sync
        def _(sp):
            sp.dma_start(xin[:], x_dram[0]).then_inc(x_loaded, 16)
            sp.dma_start(const[:], consts).then_inc(w_loaded[0], 16)
            sp.dma_start(col[:], cols).then_inc(w_loaded[1], 16)
            sp.dma_start(xb[:, 0:WS], wsmall).then_inc(w_loaded[2], 16)
            sp.dma_start(stage[1], w3).then_inc(w_loaded[3], 16)
            sp.dma_start(stage[0], w1).then_inc(w_loaded[4], 16)
            for h in range(2):
                sp.dma_start(half(res, h)[0:2 * E, :], half(sel, h)).then_inc(stored[h], 16)
            sp.dma_start(xa[0:2 * E, 0:E * H - N], sel[:, N:]).then_inc(w_loaded[6], 16)
            for k in range(3):
                sp.dma_start(b2_f[k * E:(k + 1) * E, :], b2).then_inc(w_loaded[7], 16)
            for k in range(2):
                sp.dma_start(bv_f[k:k + 1, :], bv).then_inc(w_loaded[8], 16)
            sp.dma_start(stage[2], w2).then_inc(w_loaded[5], 16)
            sp.wait_ge(split_done, 6)
            sp.dma_start(b2_h[2 * E:, :].bitcast(F32), b2_lo[2 * E:, :].bitcast(F32)).then_inc(moved, 16)
            sp.dma_start(bv_h[1:2, :].bitcast(F32), bv_lo[1:2, :].bitcast(F32)).then_inc(moved, 16)
            sp.wait_ge(x1_done, 2)
            sp.dma_start(xin[:], x_dram[1]).then_inc(x_loaded, 16)

            def turn(t, batch, following):
                sp.wait_ge(x1_done, (Count(4, 4, t)).value)
                sp.dma_start(xin[:], x_dram[following]).then_inc(x_loaded, 16)
                for h in range(2):
                    sp.wait_ge(x1_done, (Count(5 + h, 4, t)).value)
                    sp.dma_start(half(out_dram[batch], h), half(res, h)).then_inc(stored[h], 16)

            with sp.Fori(0, B - 2) as t:
                turn(t, t, t + 2)
            last = 4 * (B - 2)
            sp.wait_ge(x1_done, last + 4)
            sp.dma_start(xin[:], x_dram[0]).then_inc(x_loaded, 16)
            for h in range(2):
                sp.wait_ge(x1_done, last + 5 + h)
                sp.dma_start(half(out_dram[B - 2], h), half(res, h)).then_inc(stored[h], 16)
            for h in range(2):
                sp.wait_ge(x1_done, 4 * B - 1 + h)
                sp.dma_start(half(out_dram[B - 1], h), half(res, h)).then_inc(stored[h], 16)
            sp.wait_ge(x_loaded, 16 * (B + 1))
            for h in range(2):
                sp.wait_ge(stored[h], 16 * (B + 1))

        @block.tensor
        def _(pe):
            mm = nc.tensor.matmul

            def product(out, a_h, a_l, b_h, b_l, start=True, stop=True):
                mm(out, a_h, b_h, start=start, stop=False)
                mm(out, a_l, b_h, start=False, stop=False)
                return mm(out, a_h, b_l, start=False, stop=stop)

            def turn_x(n, h=0):
                pe.wait_ge(xn_ready, (n.i + h + 1).value)
                if h == 1:
                    pe.wait_ge(axf_done, (n.b * 2 + 1).value)
                elif n.before_kind == "ffn":
                    pe.wait_ge(rt_copied, n.before.value)
                elif n.before_kind == "att":
                    pe.wait_ge(axf_done, n.before.value)
                for k in range(TT):
                    last = nc.tensor.transpose(tile(tn, k), tile(xn, k), ident)
                last.then_inc(xt_done, 1)

            def logits(n):
                pe.wait_ge(xl_done, (n.r + 1).value)
                xh, xl = xt_h[n.r.mod(2)], xt_l[n.r.mod(2)]
                for k in range(TT):
                    last = product(tn[:, k * E:(k + 1) * E], tile(xh, k), tile(xl, k),
                                   ws_h[:, O_GW:O_GW + E], ws_l[:, O_GW:O_GW + E])
                last.then_inc(lg_done, 1)

            def turn_route(n):
                pe.wait_ge(table_step, (n.table * TABLE_STEPS + TABLE_STEPS).value)
                for k in range(TT):
                    last = nc.tensor.transpose(tile(tn, k), rw3[:, k, :], ident)
                last.then_inc(rt_done, 1)

            def down(ch, j):
                n = ch.q * NBL + j
                rt = rwt[ch.r.mod(2)]
                if j == 0:
                    mm(y[:], b2_h[:], rt[:], start=True, stop=False)
                pe.wait_ge(lo_done, (n + 1).value)
                product(y[:], tile(w2_h, j), tile(w2_l, j), p_h[n.mod(4)][:], p_l[n.mod(4)][:],
                        start=False, stop=(j == NBL - 1)).then_inc(w2_done, 1)

            def turn_y(ch):
                pe.wait_ge(ys_done, (ch.q + 1).value)
                if ch.q.due:
                    pe.wait_ge(x1_done, ch.q.value)
                for k in range(TT):
                    last = nc.tensor.transpose(tile(tp, k), tile(ys, k), ident)
                last.then_inc(yt_done, 1)

            def scores(b, m):
                h, j = divmod(m, KT)
                item = score_item(m)
                if m in (0, KT // 2, KT):
                    pe.wait_ge(kq_lo, (b * 4 + {0: 2, KT // 2: 3, KT: 4}[m]).value)
                pe.wait_ge(item_read, (b * RING + read_before(item)).value)
                product(ring[bank_of(item)][:], tile(k_h, j), tile(k_l, j), half(q_h, h), half(q_l, h))\
                    .then_inc(item_done, 1)

            def gate_product(b, k):
                hb, h = divmod(k, 2)
                item = gate_item(k)
                pe.wait_ge(item_read, (b * RING + read_before(item)).value)
                w = slice(HID + hb * P, HID + (hb + 1) * P)
                product(ring[bank_of(item)][:], ws_h[:, w], ws_l[:, w], half(ax_h, h), half(ax_l, h))\
                    .then_inc(item_done, 1)

            def values(b, m):
                h, j = divmod(m, KT)
                if h == 0 and j % 2 == 0:
                    pe.wait_ge(vl_done, (b * TT + j // 2 + 1).value)
                pe.wait_ge(al_done, (b * (2 * KT) + m + 1).value)
                for k in range(2):
                    if m == KT:
                        pe.wait_ge(og_read, (b * 4 + k + 1).value)
                    cut = slice(j * HID + k * P, j * HID + (k + 1) * P)
                    last = product(acc[k][:], v_h[:, cut], v_l[:, cut], p_h[(m + 1) % 4][:], p_l[(m + 1) % 4][:],
                                   start=(j == 0), stop=(j == KT - 1))
                last.then_inc(av_done, 1)

            def project(b, h):
                for k in range(2):
                    pe.wait_ge(o_split, (b * 4 + 2 * h + k + 1).value)
                    w = slice(O_OUT + k * D, O_OUT + (k + 1) * D)
                    last = product(zbank[h][:], ws_h[:, w], ws_l[:, w], half(o_h, k), half(o_l, k),
                                   start=(k == 0), stop=(k == 1))
                last.then_inc(z_done, 1)

            def turn_z(b, h):
                pe.wait_ge(zs_done, (b * 2 + h + 1).value)
                for k in range(TT):
                    last = nc.tensor.transpose(tile(zbank[h], k), tile(ys, k), ident)
                last.then_inc(zt_done, 1)

            def ffn(ch, before, pending, prep, following=None):
                xh, xl = xt_h[ch.r.mod(2)], xt_l[ch.r.mod(2)]
                att_b = None if before != "att" else ch.att_b
                pe.wait_ge(xl_done, (ch.r + 1).value)
                for j in range(NBL):
                    n = ch.q * NBL + j
                    if j < 2 and before == "att":
                        pe.wait_ge(item_read, (att_b * RING + RING - 2 + 2 * j).value)
                    elif j < 2 and before is None:
                        pass
                    else:
                        pe.wait_ge(g_done, (n - 1).value)
                    pair = 2 * n.mod(2)
                    product(ring[pair][:], tile(w3_h, j), tile(w3_l, j), xh[:], xl[:]).then_inc(w3_done, 1)
                    if j == 1:
                        product(ring[pair + 1][:], tile(w1_h, j), tile(w1_l, j), xh[:], xl[:]).then_inc(w1_done, 1)
                    if 1 <= j <= NR:
                        if j == 1:
                            pe.wait_ge(rt_copied, (ch.q + 1).value)
                        if j == 1 and before == "att":
                            pe.wait_ge(x2_done, (att_b * 2 + 1).value)
                        if (ch.q * NR + j - 1).due:
                            pe.wait_ge(p_done, (ch.q * NR + j - 1).value)
                        mm(rwb[:], tile(sel_sb, j - 1), rwt[ch.r.mod(2)][0:2 * E, :],
                           start=True, stop=True).then_inc(rwb_done, 1)
                    if j != 1:
                        product(ring[pair + 1][:], tile(w1_h, j), tile(w1_l, j), xh[:], xl[:]).then_inc(w1_done, 1)
                    if j >= LAG:
                        if j == LAG and before == "ffn":
                            pe.wait_ge(ys_done, ch.q.value)
                        if j == LAG and before == "att":
                            pe.wait_ge(og_read, (att_b * 4 + 3).value)
                        down(ch, j - LAG)
                    elif pending and before == "ffn":
                        down(ch.before, NBL - LAG + j)
                    elif pending and before == "att":
                        values(att_b, 2 * KT - LAG + j)
                    if j == 0:
                        turn_route(ch.norm)
                    if pending and before == "ffn" and j == 3:
                        turn_y(ch.before)
                    if pending and before == "att" and j == 8:
                        project(att_b, 1)
                    if pending and before == "att" and j == 10:
                        turn_z(att_b, 1)
                    if prep and j == (5 if prep.kind == "ffn" else 6):
                        turn_x(prep)
                    if prep and prep.kind == "att" and j == 8:
                        turn_x(prep, 1)
                    if prep and prep.kind == "ffn" and j == 7:
                        logits(prep)

            def ffn_rest(ch):
                for j in range(NBL - LAG, NBL):
                    down(ch, j)
                turn_y(ch)

            def attention(b, last_chunk, pending, prep):
                q = last_chunk.q
                for h in range(2):
                    pe.wait_ge(axl_done, (b * 2 + h + 1).value)
                    if h == 0:
                        pe.wait_ge(g_done, (q * NBL + NBL - 1).value)
                    product(ring[h][:], ws_h[:, O_QK:O_QK + D], ws_l[:, O_QK:O_QK + D],
                            half(ax_h, h), half(ax_l, h)).then_inc(item_done, 1)
                if pending:
                    down(last_chunk, NBL - 3)
                pe.wait_ge(g_done, (q * NBL + NBL).value)
                for k in range(TT):
                    item = 2 + k
                    if item >= 4:
                        pe.wait_ge(item_read, (b * RING + item - 3).value)
                    for t in range(2):
                        o = ring[bank_of(item)][:, t * HID:(t + 1) * HID]
                        xs = 2 * k + t
                        mm(o, tile(ax_h, xs), ws_h[:, 0:HID], start=True, stop=False)
                        mm(o, tile(ax_l, xs), ws_h[:, 0:HID], start=False, stop=False)
                        mm(o, tile(ax_h, xs), ws_l[:, 0:HID], start=False, stop=False)
                        last = mm(o, ones[:], bv_h[:], start=False, stop=True)
                    last.then_inc(item_done, 1)
                    if pending and k == 1:
                        down(last_chunk, NBL - 2)
                    if pending and k == 3:
                        down(last_chunk, NBL - 1)
                for m in range(2 * KT):
                    scores(b, m)
                    if m < 4:
                        gate_product(b, m)
                    if pending and m == 0:
                        turn_y(last_chunk)
                    if m == LAG:
                        pe.wait_ge(x1_done, (q + 1).value)
                    if m >= LAG:
                        values(b, m - LAG)
                    if m == 3:
                        turn_x(prep)
                    if m == 5:
                        logits(prep)
                    if m == 14:
                        project(b, 0)
                    if m == 15:
                        turn_z(b, 0)

            def attention_rest(b):
                for m in range(2 * KT - LAG, 2 * KT):
                    values(b, m)
                project(b, 1)
                turn_z(b, 1)

            link_chunks_and_run(
                pe, ffn, ffn_rest, attention, attention_rest,
                prepare=lambda n: (turn_x(n), logits(n)),
                prepare_att=lambda n: (turn_x(n), turn_x(n, 1)),
                start=lambda: (pe.wait_ge(w_loaded[0], 16), pe.wait_ge(split_done, SPLITS), pe.wait_ge(moved, 32)),
            )

        @block.scalar
        def _(act):
            act_fn = nc.scalar.activation

            def copy_x(n, h=0):
                act.wait_ge(xt_done, (n.i + h + 1).value)
                if n.kind == "ffn":
                    if (n.q * NBL).due:
                        act.wait_ge(w1_done, (n.q * NBL).value)
                    act_fn(xt_h[n.r.mod(2)][:], tn[:], ACT.Copy).then_inc(xh_done, 1)
                else:
                    if (n.b * 2 + h).due:
                        act.wait_ge(axl_done, (n.b * 2 + h).value)
                    act_fn(axf[:], tn[:], ACT.Identity, bias=c(C_LNB), scale=c(C_LNS)).then_inc(axf_done, 1)

            def silu_logits(n):
                act.wait_ge(route_step, (n.r * ROUTE_STEPS + 2).value)
                act_fn(sl[:], lg[:], ACT.Silu).then_inc(sl_done, 1)

            def copy_route(n):
                act.wait_ge(rt_done, (n.table + 1).value)
                if (n.q * NBL).due:
                    act.wait_ge(w2_done, (n.q * NBL).value)
                act_fn(rwt[n.r.mod(2)][:], tn[0:3 * E, :], ACT.Copy).then_inc(rt_copied, 1)

            def up(ch, j, before):
                n = ch.q * NBL + j
                act.wait_ge(w3_done, (n + 1).value)
                if j < 2 and before == "att":
                    act.wait_ge(a_done, (ch.att_b * (2 * KT) + 2 * KT - 1 + j).value)
                else:
                    if (n - 1).due:
                        act.wait_ge(g_done, (n - 1).value)
                act_fn(u[n.mod(2)][:], ring[2 * n.mod(2)][:], ACT.Identity, bias=c(C_B3 + j))\
                    .then_inc(u_done, 1)

            def silu(ch, j):
                n = ch.q * NBL + j
                act.wait_ge(g_done, (n + 1).value)
                if j < NR:
                    act_fn(g[n.mod(4)][:], g[n.mod(4)][:], ACT.Silu).then_inc(s_done, 1)
                else:
                    act.wait_ge(lo_done, (n - 1).value)
                    act_fn(p[n.mod(2)][:], g[n.mod(4)][:], ACT.Silu).then_inc(s_done, 1)

            def high(ch, j, before=None):
                n = ch.q * NBL + j
                if j < NR:
                    act.wait_ge(p_done, (ch.q * NR + j + 1).value)
                else:
                    act.wait_ge(s_done, (n + 1).value)
                if j < 4 and before == "att":
                    act.wait_ge(av_done, (ch.att_b * (2 * KT) + min(2 * KT - 2 + j, 2 * KT)).value)
                else:
                    if (n - 3).due:
                        act.wait_ge(w2_done, (n - 3).value)
                act_fn(p_h[n.mod(4)][:], p[n.mod(2)][:], ACT.Copy).then_inc(hi_done, 1)

            def half_y(ch):
                act.wait_ge(w2_done, (ch.q * NBL + NBL).value)
                if ch.q.due:
                    act.wait_ge(yt_done, ch.q.value)
                act_fn(ys[:], y[:], ACT.Identity, bias=hb2[:, 0:1], scale=0.5).then_inc(ys_done, 1)

            def ffn(ch, before, pending, prep, following=None):
                for j in range(NBL):
                    if pending and before == "ffn" and j == 3:
                        half_y(ch.before)
                    if prep and prep.kind == "ffn" and j == 9:
                        silu_logits(prep)
                    if j >= 1:
                        silu(ch, j - 1)
                    elif pending and before == "ffn":
                        silu(ch.before, NBL - 1)
                    up(ch, j, before)
                    if prep and j == (6 if prep.kind == "ffn" else 7):
                        copy_x(prep)
                    if prep and prep.kind == "att" and j == 9:
                        copy_x(prep, 1)
                    if j >= 1:
                        high(ch, j - 1, before)
                    elif pending and before == "ffn":
                        high(ch.before, NBL - 1)
                    if j == 0:
                        copy_route(ch.norm)
                    if pending and before == "att" and j == 9:
                        bias_z(ch.att_b, 1)

            def ffn_rest(ch):
                silu(ch, NBL - 1)
                high(ch, NBL - 1)
                half_y(ch)

            def bias_z(b, h):
                act.wait_ge(z_done, (b * 2 + h + 1).value)
                if h == 0:
                    act.wait_ge(yt_done, (ys_uses_before(b)).value)
                else:
                    act.wait_ge(zt_done, (b * 2 + 1).value)
                act_fn(ys[:], zbank[h][:], ACT.Identity, bias=c(C_BO)).then_inc(zs_done, 1)

            def item(b, k):
                act.wait_ge(item_done, (b * RING + k + 1).value)
                bank = ring[bank_of(k)]
                if k < 2:
                    if (b * 4).due:
                        act.wait_ge(kqf_done, (b * 4).value)
                    act_fn(half(qkf, k), bank[:], ACT.Silu, bias=c(C_BQK)).then_inc(item_read, 1)
                elif k < 2 + TT:
                    if (b * TT + k - 2 - 1).due:
                        act.wait_ge(vl_done, (b * TT + k - 2 - 1).value)
                    act_fn(half(vf, k % 2), bank[:], ACT.Silu).then_inc(item_read, 1)
                else:
                    kk = (k - SIM0) // 2
                    if (b * 4).due:
                        act.wait_ge(og_read, (b * 4).value)
                    act_fn(gate[:, kk * HALF:(kk + 1) * HALF], bank[:], ACT.Silu,
                           bias=c(C_BG + kk // 2)).then_inc(item_read, 1)

            def relu(b, m):
                act.wait_ge(item_done, (b * RING + score_item(m) + 1).value)
                if m < 2:
                    act.wait_ge(g_done, (after_ffn(b)).value)
                else:
                    act.wait_ge(a_done, (b * (2 * KT) + m - 1).value)
                act_fn(u[m % 2][:], ring[bank_of(score_item(m))][:], ACT.Relu, scale=1.0 / N).then_inc(item_read, 1)

            def attention(b, last_chunk, pending, prep):
                if pending:
                    silu(last_chunk, NBL - 1)
                item(b, 0)
                if pending:
                    high(last_chunk, NBL - 1)
                item(b, 1)
                for k in range(2, 2 + TT):
                    item(b, k)
                if pending:
                    half_y(last_chunk)
                for m in range(2 * KT):
                    relu(b, m)
                    if m < 4:
                        item(b, gate_item(m))
                    if m == 3:
                        copy_x(prep)
                    if m == 7:
                        silu_logits(prep)
                    if m == 15:
                        bias_z(b, 0)

            def start():
                for dst, src, k in ((ws_h[:], xb[:, 0:WS], 2), (w3_h[:], stage[1], 3), (w1_h[:], stage[0], 4),
                                    (w2_h[:], stage[2], 5)):
                    act.wait_ge(w_loaded[k], 16)
                    act_fn(dst, src, ACT.Copy).then_inc(copies_done, 1)
                act.wait_ge(split_done, SPLITS)

            link_chunks_and_run(
                act, ffn, ffn_rest, attention, lambda b: bias_z(b, 1),
                prepare=lambda n: (copy_x(n), silu_logits(n)),
                prepare_att=lambda n: (copy_x(n), copy_x(n, 1)),
                start=start,
            )

        @block.vector
        def _(dve):
            v = nc.vector

            def sources(n):
                return {"xin": xin, "xa": xa, "xb": xb}[n.source]

            def norm(n, part):
                at = n.u * NORM_STEPS
                src = sources(n)
                tiles = TT * len(n.halves)
                if n.kind == "ffn":
                    src = half(src, n.half)
                if part == 0:
                    if at.due:
                        dve.wait_ge(norm_step, at.value)
                    if n.source == "xin" and n.half == 0:
                        dve.wait_ge(x_loaded, ((n.b + 1) * 16).value)
                    if n.source == "xa":
                        dve.wait_ge(x1_done, (n.q_of_source + 1).value)
                    if n.source == "xb":
                        dve.wait_ge(x2_done, (n.b * 2 + n.half + 1).value)
                    for k in range(TT):
                        last = v.bn_stats(st[:, k, :], tile(src, k))
                    if n.kind == "ffn":
                        last.then_inc(norm_step, 1)
                elif part == "second":
                    for k in range(TT, tiles):
                        last = v.bn_stats(st[:, k, :], tile(src, k))
                    last.then_inc(norm_step, 1)
                elif part == 1:
                    if n.i.due:
                        dve.wait_ge(xn_ready, n.i.value)
                    dve.wait_ge(norm_step, (at + 1).value)
                    dve.sem_inc(passed_dve, 1)
                    for k in range(tiles):
                        last = v.bn_aggr(mv[:, k, :], st[:, k, :])
                    last.then_inc(norm_step, 1)
                elif part == 2:
                    dve.wait_ge(norm_step, (at + 2).value)
                    one, two = (1.0, EPS) if n.kind == "ffn" else (1.0 + EPS, EPS * EPS)
                    v.tensor_scalar(vv[:, 0:tiles], mv[:, 0:tiles, 1], one, two, ALU.mult, ALU.add).then_inc(norm_step, 1)
                    dve.wait_ge(norm_step, (at + 3).value)
                    v.tensor_scalar(ri[:, 0:tiles], vv[:, 0:tiles].bitcast(I32), 1, None, ALU.logical_shift_right)\
                        .then_inc(norm_step, 1)
                    dve.wait_ge(norm_step, (at + 4).value)
                    v.tensor_scalar(ri[:, 0:tiles], ri[:, 0:tiles], -1.0, float(0x5F3759DF), ALU.mult, ALU.add)\
                        .then_inc(norm_step, 1)
                elif part <= 5:
                    k = at + 5 + 3 * (part - 3)
                    r, t1_, t2_ = ri[:, 0:tiles].bitcast(F32), t1[:, 0:tiles], t2[:, 0:tiles]
                    dve.wait_ge(norm_step, k.value)
                    v.scalar_tensor_tensor(t1_, r, -0.5, r, ALU.mult, ALU.mult).then_inc(norm_step, 1)
                    dve.wait_ge(norm_step, (k + 1).value)
                    v.tensor_tensor(t2_, t1_, vv[:, 0:tiles], ALU.mult).then_inc(norm_step, 1)
                    dve.wait_ge(norm_step, (k + 2).value)
                    v.scalar_tensor_tensor(r, t2_, 1.5, r, ALU.add, ALU.mult).then_inc(norm_step, 1)
                else:
                    h = part - 6
                    dve.wait_ge(norm_step, (at + NORM_STEPS).value)
                    if (n.i + h).due:
                        dve.wait_ge(xt_done, (n.i + h).value)
                    for k in range(TT):
                        t = h * TT + k
                        last = v.tensor_scalar(tile(xn, k), tile(src, t), mv[:, t, 0:1],
                                               ri[:, t:t + 1].bitcast(F32), ALU.subtract, ALU.mult)
                    last.then_inc(xn_ready, 1)

            def low_x(n):
                dve.wait_ge(xh_done, (n.r + 1).value)
                k = n.r.mod(2)
                v.tensor_tensor(xt_l[k][:], tn[:], xt_h[k][:].bitcast(F32), ALU.subtract).then_inc(xl_done, 1)

            def high_ax(n, h):
                dve.wait_ge(axf_done, (n.b * 2 + h + 1).value)
                v.tensor_copy(half(ax_h, h), axf[:]).then_inc(axh_done, 1)

            def wide(t):
                return t[:].unsqueeze(2).to_broadcast([P, TT, E])

            def route(n, part):
                at = n.r * ROUTE_STEPS
                if part == 0:
                    l3 = tn[:, 0:TT * E].rearrange("p (t e) -> p t e", e=E)
                    if at.due:
                        dve.wait_ge(route_step, at.value)
                    dve.wait_ge(lg_done, (n.r + 1).value)
                    v.tensor_reduce(mx[:], l3, AX.X, ALU.max).then_inc(route_step, 1)
                    dve.wait_ge(route_step, (at + 1).value)
                    v.tensor_tensor(lg[:], l3, wide(mx), ALU.subtract).then_inc(route_step, 1)
                elif part == 1:
                    dve.wait_ge(sl_done, (n.r + 1).value)
                    v.scalar_tensor_tensor(dn[:], lg[:], TINY, sl[:], ALU.subtract, ALU.subtract)\
                        .then_inc(route_step, 1)
                    dve.wait_ge(route_step, (at + 3).value)
                    v.reciprocal(dn[:], dn[:]).then_inc(route_step, 1)
                    dve.wait_ge(route_step, (at + 4).value)
                    v.scalar_tensor_tensor(ex[:], sl[:], TINY, dn[:], ALU.subtract, ALU.mult)\
                        .then_inc(route_step, 1)
                elif part == 2:
                    dve.wait_ge(route_step, (at + 5).value)
                    v.tensor_reduce(sm[:], ex[:], AX.X, ALU.add).then_inc(route_step, 1)
                    dve.wait_ge(route_step, (at + 6).value)
                    v.reciprocal(rc[:], sm[:]).then_inc(route_step, 1)
                    dve.wait_ge(route_step, (at + 7).value)
                    v.tensor_tensor(sc[:], ex[:], wide(rc), ALU.mult).then_inc(route_step, 1)
                    dve.wait_ge(route_step, (at + 8).value)
                    gb = col[:, C_GB:C_GB + E].unsqueeze(1).to_broadcast([P, TT, E])
                    v.tensor_tensor(bi[:], sc[:], gb, ALU.add).then_inc(route_step, 1)
                elif part == 3:
                    mine = bi[:].unsqueeze(3).to_broadcast([P, TT, E, E])
                    other = bi[:].unsqueeze(2).to_broadcast([P, TT, E, E])
                    first = before.unsqueeze(1).to_broadcast([P, TT, E * E])
                    dve.wait_ge(route_step, (at + 9).value)
                    v.tensor_tensor(diff[:].rearrange("p t (e f) -> p t e f", f=E), other, mine, ALU.subtract)\
                        .then_inc(route_step, 1)
                    dve.wait_ge(route_step, (at + 10).value)
                    v.scalar_tensor_tensor(eq[:], diff[:], 0.0, first, ALU.is_equal, ALU.mult)\
                        .then_inc(route_step, 1)
                elif part == 4:
                    dve.wait_ge(route_step, (at + 11).value)
                    v.scalar_tensor_tensor(gt[:], diff[:], 0.0, eq[:], ALU.is_gt, ALU.add).then_inc(route_step, 1)
                    dve.wait_ge(route_step, (at + 12).value)
                    v.tensor_reduce(rank[:], gt[:].rearrange("p t (e f) -> p t e f", f=E), AX.X, ALU.add)\
                        .then_inc(route_step, 1)
                elif part == 5:
                    made = n.table * TABLE_STEPS
                    if made.due:
                        dve.wait_ge(table_step, made.value)
                    dve.wait_ge(route_step, (at + 13).value)
                    v.scalar_tensor_tensor(rw[:], rank[:], 2.0, sc[:], ALU.is_lt, ALU.mult).then_inc(table_step, 1)
                    dve.wait_ge(table_step, (made + 1).value)
                    v.tensor_copy(rwh[:], rw[:]).then_inc(table_step, 1)
                else:
                    dve.wait_ge(table_step, (n.table * TABLE_STEPS + 2).value)
                    if n.table.due:
                        dve.wait_ge(rt_done, n.table.value)
                    high = rwh[:].bitcast(F32).unsqueeze(2).to_broadcast([P, TT, 2, E])
                    v.tensor_copy(rw3[:, :, 0:4 * E].rearrange("p t (k e) -> p t k e", e=2 * E)[:, :, :, 0:E], high)\
                        .then_inc(table_step, 1)
                    v.tensor_tensor(rw3[:, :, E:2 * E], rw[:], rwh[:].bitcast(F32), ALU.subtract)\
                        .then_inc(table_step, 1)

            def product(ch, j, before):
                n = ch.q * NBL + j
                dve.wait_ge(w1_done, (n + 1).value)
                dve.wait_ge(u_done, (n + 1).value)
                if j < 4 and before == "att":
                    dve.wait_ge(al_done, (ch.att_b * (2 * KT) + min(2 * KT - 2 + j, 2 * KT)).value)
                else:
                    if (n - 3).due:
                        dve.wait_ge(s_done, (n - 3).value)
                    done = ch.q * NR + max(j - 3, 0)
                    if done.due:
                        dve.wait_ge(p_done, done.value)
                v.scalar_tensor_tensor(g[n.mod(4)][:], ring[2 * n.mod(2) + 1][:], c(C_B1 + j), u[n.mod(2)][:],
                                       ALU.add, ALU.mult).then_inc(g_done, 1)

            def weigh(ch, j):
                n = ch.q * NBL + j
                dve.wait_ge(s_done, (n + 1).value)
                dve.wait_ge(rwb_done, (ch.q * NR + j + 1).value)
                if (n - 1).due:
                    dve.wait_ge(lo_done, (n - 1).value)
                v.tensor_tensor(p[n.mod(2)][:], g[n.mod(4)][:], rwb[:], ALU.mult).then_inc(p_done, 1)

            def residual(ch):
                dve.wait_ge(yt_done, (ch.q + 1).value)
                src, dst = (xin, xa) if ch.ffn == 1 else (xb, res)
                if ch.ffn == 2:
                    dve.wait_ge(stored[ch.half], (ch.b * 16 + 16).value)
                else:
                    if (ch.b * 2 + ch.half - 1).due:
                        dve.wait_ge(x2_done, (ch.b * 2 + ch.half - 1).value)
                v.tensor_tensor(half(dst, ch.half), half(src, ch.half), tp[:], ALU.add).then_inc(x1_done, 1)

            def gate_o(b, h, part):
                dve.wait_ge(av_done, (b * (2 * KT) + (h + 1) * KT).value)
                dve.wait_ge(item_read, (b * RING + gate_item(3) + 1).value)
                if (b * 4 + 2 * h).due:
                    dve.wait_ge(o_split, (b * 4 + 2 * h).value)
                v.tensor_tensor(half(o_f, part), acc[part][:],
                                gate[:, (2 * part + h) * HALF:(2 * part + h + 1) * HALF], ALU.mult).then_inc(og_read, 1)

            def split_o(b, h, part):
                if part == 0:
                    dve.wait_ge(og_read, (b * 4 + 2 * h + 2).value)
                    if (b * 2 + h).due:
                        dve.wait_ge(z_done, (b * 2 + h).value)
                    v.tensor_copy(o_h[:], o_f[:]).then_inc(oh_done, 1)
                else:
                    dve.wait_ge(oh_done, (b * 2 + h + 1).value)
                    for k in range(2):
                        v.tensor_tensor(half(o_l, k), half(o_f, k), half(o_h, k).bitcast(F32), ALU.subtract)\
                            .then_inc(o_split, 1)

            def residual_z(b, h):
                dve.wait_ge(zt_done, (b * 2 + h + 1).value)
                dve.wait_ge(x1_done, (b * 4 + h + 1).value)
                v.tensor_tensor(half(xb, h), half(xa, h), zbank[h][:], ALU.add).then_inc(x2_done, 1)

            def ffn(ch, before, pending, prep, following=None):
                for j in range(NBL):
                    if j == 0 and ch.norm.after_att:
                        route(ch.norm, 5)
                        if pending:
                            residual_z(ch.att_b, 0)
                        route(ch.norm, 6)
                    if pending and before == "att" and j == 3:
                        gate_o(ch.att_b, 1, 0)
                    if 1 <= j <= NR:
                        weigh(ch, j - 1)
                    if prep and prep.kind == "ffn" and j == 12:
                        route(prep, 4)
                    product(ch, j, before)
                    if pending and before == "ffn" and j == 5:
                        residual(ch.before)
                    if pending and before == "att":
                        if j == 3:
                            gate_o(ch.att_b, 1, 1)
                        if j == 5:
                            split_o(ch.att_b, 1, 0)
                        if j == 11:
                            residual_z(ch.att_b, 1)
                    if prep and prep.kind == "ffn":
                        for part in {0: (0,), 1: (1, 2), 2: (3,), 3: (4, 5), 4: (6,)}.get(j, ()):
                            norm(prep, part)
                        if j == 6:
                            low_x(prep)
                        if 8 <= j < 12:
                            route(prep, j - 8)
                        if j == 12:
                            route(prep, 5)
                            route(prep, 6)
                    if prep and prep.kind == "att":
                        for part in {0: (0,), 1: ("second",), 2: (1, 2), 3: (3, 4), 4: (5,), 5: (6,), 7: (7,)}.get(j, ()):
                            norm(prep, part)
                        if j in (7, 10):
                            high_ax(prep, j // 10)
                        for part in {10: (0,), 11: (1, 2), 12: (3, 4, 5)}.get(j, ()):
                            norm(following, part)

            def kq(b, k):
                dve.wait_ge(item_read, (b * RING + k // 2 + 1).value)
                if (b * 4 + k - 1).due:
                    dve.wait_ge(kq_lo, (b * 4 + k - 1).value)
                w, bb = (C_KW, C_KB) if k % 2 == 0 else (C_QW, C_QB)
                v.tensor_scalar(half(kqt, k % 2), half(qkf, k // 2), c(w), c(bb), ALU.mult, ALU.add)\
                    .then_inc(kqf_done, 1)
                dve.wait_ge(kqf_done, (b * 4 + k + 1).value)
                v.tensor_copy(half((k_h, q_h)[k % 2], k // 2), half(kqt, k % 2)).then_inc(kq_hi, 1)

            def split_v(b, k):
                cut = slice(k * HALF, (k + 1) * HALF)
                dve.wait_ge(item_read, (b * RING + 2 + k + 1).value)
                v.tensor_copy(v_h[:, cut], half(vf, k % 2)).then_inc(vh_done, 1)
                dve.wait_ge(vh_done, (b * TT + k + 1).value)
                v.tensor_tensor(v_l[:, cut], half(vf, k % 2), v_h[:, cut].bitcast(F32), ALU.subtract)\
                    .then_inc(vl_done, 1)

            def square(b, m):
                dve.wait_ge(item_read, (b * RING + score_item(m) + 1).value)
                if m == 0:
                    dve.wait_ge(s_done, (after_ffn(b)).value)
                    dve.wait_ge(w2_done, (after_ffn(b)).value)
                    dve.wait_ge(p_done, (b * (4 * NR) + 2 * NR).value)
                if m >= 4:
                    dve.wait_ge(al_done, (b * (2 * KT) + m - 3).value)
                v.tensor_tensor(g[(m + 1) % 4][:], u[m % 2][:], u[m % 2][:], ALU.mult).then_inc(a_done, 1)
                dve.wait_ge(a_done, (b * (2 * KT) + m + 1).value)
                if m >= 4:
                    dve.wait_ge(av_done, (b * (2 * KT) + m - 3).value)
                v.tensor_copy(p_h[(m + 1) % 4][:], g[(m + 1) % 4][:]).then_inc(ah_done, 1)

            def attention(b, last_chunk, pending, prep):
                if not pending:
                    for part in range(6):
                        norm(prep, part)
                kq(b, 0)
                kq(b, 1)
                for k in range(TT):
                    split_v(b, k)
                kq(b, 2)
                for m in range(2 * KT):
                    if m == 10:
                        gate_o(b, 0, 0)
                        gate_o(b, 0, 1)
                    square(b, m)
                    if m == 2:
                        norm(prep, 6)
                    if m == 3:
                        kq(b, 3)
                    if pending and m == 1:
                        residual(last_chunk)
                    if m == 4:
                        low_x(prep)
                    if 6 <= m <= 9:
                        route(prep, m - 6)
                    if m in (11, 12):
                        split_o(b, 0, m - 11)
                    if m == 13:
                        route(prep, 4)

            def attention_rest(b):
                residual_z(b, 0)
                gate_o(b, 1, 0)
                gate_o(b, 1, 1)
                split_o(b, 1, 0)
                residual_z(b, 1)

            def prepare(n):
                for k in range(7):
                    norm(n, k)
                low_x(n)
                for k in range(7):
                    route(n, k)

            def prepare_att(n):
                for k in (0, "second", 1, 2, 3, 4, 5, 6, 7):
                    norm(n, k)
                    if k == 6:
                        high_ax(n, 0)
                high_ax(n, 1)

            def start():
                dve.wait_ge(w_loaded[1], 16)
                v.tensor_scalar(hb2[:], c(C_SB2), 0.5, None, ALU.mult).then_inc(split_done, 1)
                v.memset(rw3[:], 0.0).then_inc(split_done, 1)
                dve.wait_ge(w_loaded[0], 16)
                v.tensor_copy(ones[:], ones_f).then_inc(split_done, 1)
                dve.wait_ge(w_loaded[7], 48)
                dve.wait_ge(w_loaded[8], 32)
                v.tensor_copy(b2_h[:], b2_f[:])
                v.tensor_copy(bv_h[:], bv_f[:]).then_inc(split_done, 1)
                dve.wait_ge(split_done, 4)
                v.tensor_tensor(b2_lo[:], b2_f[:], b2_h[:].bitcast(F32), ALU.subtract).then_inc(split_done, 1)
                v.tensor_tensor(bv_lo[:], bv_f[:], bv_h[:].bitcast(F32), ALU.subtract).then_inc(split_done, 1)
                dve.wait_ge(w_loaded[6], 16)
                dve.wait_ge(stored[0], 16)
                dve.wait_ge(stored[1], 16)
                v.tensor_copy(sel_sb[:, 0:N], res[0:2 * E, 0:N])
                v.tensor_copy(sel_sb[:, N:], xa[0:2 * E, 0:E * H - N]).then_inc(split_done, 1)
                for k, (dst, src, hi) in enumerate(((ws_l[:], xb[:, 0:WS], ws_h), (w3_l[:], stage[1], w3_h),
                                                    (w1_l[:], stage[0], w1_h), (w2_l[:], stage[2], w2_h))):
                    dve.wait_ge(copies_done, k + 1)
                    v.tensor_tensor(dst, src, hi[:].bitcast(F32), ALU.subtract).then_inc(split_done, 1)

            link_chunks_and_run(dve, ffn, residual, attention, attention_rest,
                                prepare=prepare, prepare_att=prepare_att, start=start)

        @block.gpsimd
        def _(pool):
            gp = nc.gpsimd

            def low(ch, j):
                n = ch.q * NBL + j
                pool.wait_ge(hi_done, (n + 1).value)
                gp.tensor_tensor(p_l[n.mod(4)][:], p[n.mod(2)][:], p_h[n.mod(4)][:].bitcast(F32),
                                 ALU.subtract).then_inc(lo_done, 1)

            def low_ax(n, h):
                pool.wait_ge(axh_done, (n.b * 2 + h + 1).value)
                gp.tensor_tensor(half(ax_l, h), axf[:], half(ax_h, h).bitcast(F32), ALU.subtract)\
                    .then_inc(axl_done, 1)

            def ffn(ch, before, pending, prep, following=None):
                for j in range(NBL):
                    if j >= 1:
                        low(ch, j - 1)
                    elif pending and before == "ffn":
                        low(ch.before, NBL - 1)
                    if prep and prep.kind == "att" and j in (8, 11):
                        low_ax(prep, j // 11)
                    if pending and before == "att" and j in (5, 6):
                        low_o(ch.att_b, 1, j - 5)

            def ffn_rest(ch):
                low(ch, NBL - 1)

            def low_o(b, h, k):
                pool.wait_ge(oh_done, (b * 2 + h + 1).value)
                gp.tensor_tensor(half(o_l, k), half(o_f, k), half(o_h, k).bitcast(F32), ALU.subtract)\
                    .then_inc(o_split, 1)

            def low_kq(b, k):
                pool.wait_ge(kq_hi, (b * 4 + k + 1).value)
                hi, lo = ((k_h, k_l), (q_h, q_l))[k % 2]
                gp.tensor_tensor(half(lo, k // 2), half(kqt, k % 2), half(hi, k // 2).bitcast(F32),
                                 ALU.subtract).then_inc(kq_lo, 1)

            def low_a(b, m):
                pool.wait_ge(ah_done, (b * (2 * KT) + m + 1).value)
                k = (m + 1) % 4
                gp.tensor_tensor(p_l[k][:], g[k][:], p_h[k][:].bitcast(F32), ALU.subtract).then_inc(al_done, 1)

            def attention(b, last_chunk, pending, prep):
                low_kq(b, 0)
                if pending:
                    low(last_chunk, NBL - 1)
                low_kq(b, 1)
                low_kq(b, 2)
                for m in range(2 * KT):
                    low_a(b, m)
                    if m == 3:
                        low_kq(b, 3)

            def attention_rest(b):
                low_o(b, 1, 0)
                low_o(b, 1, 1)

            link_chunks_and_run(pool, ffn, ffn_rest, attention, attention_rest,
                                prepare=lambda n: None, prepare_att=lambda n: (low_ax(n, 0), low_ax(n, 1)),
                                start=lambda: pool.wait_ge(w_loaded[0], 16))


SPLITS = 11


def after_ffn(b):
    return b * (4 * NBL) + 2 * NBL


def ys_uses_before(b):
    return b * 4 + 2


def link_chunks_and_run(eng, ffn, ffn_rest, attention, attention_rest, prepare, prepare_att, start):
    def follow(n, before_kind, before):
        n.before_kind, n.before = before_kind, before
        return n

    start()
    c, first, second, att, following = phases_before()
    c[1].before = c[0]
    follow(first, None, None)
    follow(second, "ffn", Count(1))
    follow(att, "ffn", Count(2))
    follow(following, "att", Count(2))
    att.q_of_source = Count(1)
    c[0].norm, c[1].norm = first, second
    prepare(first)
    ffn(c[0], None, False, second)
    ffn(c[1], "ffn", True, None)
    ffn_rest(c[1])
    prepare_att(att)
    attention(Count(0), c[1], False, following)

    with eng.Fori(0, B - 1) as turn:
        c, preps, b, following = phases_of_turn(turn)
        for k in range(1, 4):
            c[k].before = c[k - 1]
        c[0].att_b = b - 1
        for k in range(4):
            follow(preps[k], "ffn", c[k].r + 1)
            c[k].norm = preps[k - 1]
        c[0].norm = Norm(None, None, "ffn", "xin", b, 0, c[0].r, c[0].q - 1)
        c[0].norm.after_att = True
        follow(following, "att", b * 2 + 2)
        preps[3].q_of_source = c[1].q
        ffn(c[0], "att", True, preps[0])
        for k in range(1, 4):
            ffn(c[k], "ffn", True, preps[k], following)
        attention(b, c[3], True, following)

    c, first, second = phases_after()
    c[0].att_b = Count(B - 1)
    c[1].before = c[0]
    follow(first, "ffn", c[0].q)
    follow(second, "ffn", c[1].q)
    attention_rest(Count(B - 1))
    c[0].norm, c[1].norm = first, second
    prepare(first)
    ffn(c[0], "att", False, second)
    ffn(c[1], "ffn", True, None)
    ffn_rest(c[1])


def kernel(L0_attn_x, L0_attn_ln_scale, L0_attn_ln_bias, L0_attn_W_hidden, L0_attn_b_hidden, L0_attn_W_qk,
           L0_attn_b_qk, L0_attn_os_weight, L0_attn_os_bias, L0_attn_W_out, L0_attn_b_out, L0_ffn_gate_w,
           L0_ffn_gate_b, L0_ffn_w1, L0_ffn_b1, L0_ffn_w3, L0_ffn_b3, L0_ffn_w2, L0_ffn_b2, L0_ffn_sw1,
           L0_ffn_sb1, L0_ffn_sw3, L0_ffn_sb3, L0_ffn_sw2, L0_ffn_sb2):
    import concourse.bacc as bacc
    from concourse.bass_utils import run_bass_kernel_spmd

    def arr(a):
        return np.ascontiguousarray(a)

    def blocks(flat):
        pad = np.zeros((HW - flat.shape[-1],), flat.dtype) if flat.ndim == 1 else \
            np.zeros((flat.shape[0], HW - flat.shape[-1]), flat.dtype)
        return np.concatenate([flat, pad], axis=-1)

    def wide(w, sw):
        w = arr(w)
        return blocks(np.concatenate([w.transpose(1, 0, 2).reshape(D, E * H), arr(sw)], axis=1))

    def by_block(b, sb):
        return blocks(np.concatenate([arr(b).reshape(-1), arr(sb)])).reshape(NBL, P).T

    down = np.concatenate([arr(L0_ffn_w2).reshape(E * H, D), arr(L0_ffn_sw2)], axis=0)
    down = blocks(arr(down.T)).T.reshape(NBL, P, D).transpose(1, 0, 2).reshape(P, HW)
    osw, osb, bh = arr(L0_attn_os_weight), arr(L0_attn_os_bias), arr(L0_attn_b_hidden)
    one_cols = [L0_ffn_sb2, L0_attn_ln_scale, L0_attn_ln_bias, L0_attn_b_qk, bh[HID:HID + P], bh[HID + P:],
                osw[0], osw[1], osb[0], osb[1], L0_attn_b_out]
    cols = np.concatenate([by_block(L0_ffn_b1, L0_ffn_sb1), by_block(L0_ffn_b3, L0_ffn_sb3)]
                          + [arr(a).reshape(P, 1) for a in one_cols]
                          + [np.repeat(arr(L0_ffn_gate_b).reshape(1, E), P, axis=0)], axis=1)
    before = np.tril(np.ones((E, E), np.float32), -1).reshape(1, E * E)
    consts = np.concatenate([np.eye(P, dtype=np.float32), np.repeat(before, P, axis=0),
                             np.ones((P, P), np.float32)], axis=1)
    sel = np.repeat(np.tile(np.eye(E, dtype=np.float32), (2, 1)), H, axis=1)
    wo = arr(L0_attn_W_out).reshape(2, P, D).transpose(1, 0, 2).reshape(P, 2 * D)
    wsmall = np.concatenate([arr(L0_attn_W_hidden), arr(L0_attn_W_qk), wo, arr(L0_ffn_gate_w).T], axis=1)
    arrays = {
        "x": arr(L0_attn_x), "cols": arr(cols), "consts": arr(consts), "sel": arr(sel),
        "w1": arr(wide(L0_ffn_w1, L0_ffn_sw1)), "w3": arr(wide(L0_ffn_w3, L0_ffn_sw3)), "w2": arr(down),
        "wsmall": arr(wsmall), "b2": arr(L0_ffn_b2), "bv": arr(bh[:HID].reshape(1, HID)),
    }
    nc = bacc.Bacc("TRN2", target_bir_lowering=False, num_devices=1)
    args = [nc.dram_tensor(k, a.shape, mybir.dt.from_np(a.dtype), kind="ExternalInput").ap()
            for k, a in arrays.items()]
    out = nc.dram_tensor("out", (B, N, D), F32, kind="ExternalOutput").ap()
    build(nc, *args, out)
    got = run_bass_kernel_spmd(nc, [arrays], core_ids=[0])
    return got.results[0]["out"]
```

```python
from contextlib import ExitStack

import numpy as np

import concourse.bass as bass
from concourse import mybir

F32 = mybir.dt.float32
F32R = mybir.dt.float32r
I32 = mybir.dt.int32
ALU = mybir.AluOpType
ACT = mybir.ActivationFunctionType
AX = mybir.AxisListType

B, N, D = 8, 1024, 128
E, H, HID = 8, 176, 256
P = 128
HALF = N // 2
TT = HALF // P
NR = E * H // P
NBL = -(-(E + 1) * H // P)
HW = NBL * P
KT = N // P
RING = 2 + TT + 4 + 2 * KT
SIM0 = 2 + TT
LAG = 3
NORM_STEPS, ROUTE_STEPS, TABLE_STEPS = 14, 13, 4
EPS = 1e-5
TINY = 2.0 ** -120

C_B1, C_B3 = 0, NBL
C_SB2 = 2 * NBL
C_LNS, C_LNB, C_BQK, C_BG = C_SB2 + 1, C_SB2 + 2, C_SB2 + 3, C_SB2 + 4
C_QW, C_KW, C_QB, C_KB = C_BG + 2, C_BG + 3, C_BG + 4, C_BG + 5
C_BO = C_BG + 6
C_GB = C_BO + 1
NCOL = C_GB + E


class Count:

    def __init__(self, first, step=0, turn=None):
        self.first, self.step, self.turn = first, step, turn

    def __add__(self, k):
        return Count(self.first + k, self.step, self.turn)

    def __sub__(self, k):
        return self + -k

    def __mul__(self, k):
        return Count(self.first * k, self.step * k, self.turn)

    @property
    def due(self):
        return self.turn is not None or self.first > 0

    @property
    def value(self):
        assert self.first > 0
        return self.first if self.turn is None else self.turn * self.step + self.first

    def mod(self, m):
        assert self.step % m == 0
        return self.first % m


class Chunk:

    def __init__(self, q, r, b, half, ffn):
        self.q, self.r, self.b, self.half, self.ffn = q, r, b, half, ffn


class Norm:

    def __init__(self, u, i, kind, source, b, half, r=None, q=None):
        self.u, self.i, self.kind, self.source, self.b, self.half, self.r, self.q = u, i, kind, source, b, half, r, q
        self.table = r
        self.after_att = False
        self.halves = (half,) if kind == "ffn" else (0, 1)


def score_item(m):
    return SIM0 + m + min(m + 1, 4)


def gate_item(k):
    return SIM0 + 2 * k


def bank_of(item):
    return (item if item < SIM0 else item + 2) % 4


def read_before(item):
    return item - 3 if item < SIM0 or item >= SIM0 + 2 else item - 1


def phases_before():
    c = [Chunk(Count(k), Count(k), Count(0), k, 1) for k in range(2)]
    first = Norm(Count(0), Count(0), "ffn", "xin", Count(0), 0, Count(0), Count(-1))
    second = Norm(Count(1), Count(1), "ffn", "xin", Count(0), 1, Count(1), Count(0))
    att = Norm(Count(2), Count(2), "att", "xa", Count(0), 0)
    following = Norm(Count(3), Count(4), "ffn", "xin", Count(1), 0, Count(2), Count(1))
    return c, first, second, att, following


def phases_of_turn(turn):
    q, u, i = Count(2, 4, turn), Count(4, 5, turn), Count(5, 6, turn)
    b, last = Count(1, 1, turn), Count(0, 1, turn)
    c = [Chunk(q + k, q + k, b if k < 2 else last, k % 2, 1 if k < 2 else 2) for k in range(4)]
    preps = [
        Norm(u, i, "ffn", "xin", b, 1, q + 1, q),
        Norm(u + 1, i + 1, "ffn", "xb", last, 0, q + 2, q + 1),
        Norm(u + 2, i + 2, "ffn", "xb", last, 1, q + 3, q + 2),
        Norm(u + 3, i + 3, "att", "xa", b, 0),
    ]
    following = Norm(u + 4, i + 5, "ffn", "xin", b + 1, 0, q + 4, q + 3)
    return c, preps, b, following


def phases_after():
    q, u, i, b = 4 * B - 2, 5 * B - 1, 6 * B - 1, Count(B - 1)
    c = [Chunk(Count(q + k), Count(q + 1 + k), b, k, 2) for k in range(2)]
    first = Norm(Count(u), Count(i), "ffn", "xb", b, 0, Count(q + 1), Count(q))
    second = Norm(Count(u + 1), Count(i + 1), "ffn", "xb", b, 1, Count(q + 2), Count(q))
    first.table, second.table = c[0].q, c[1].q
    return c, first, second


def build(nc, x, cols, consts, sel, w1, w3, w2, wsmall, b2, bv, out):
    with ExitStack() as ctx:
        def sb(name, shape, dt=F32):
            return ctx.enter_context(nc.sbuf_tensor(name, shape, dt))

        def sem(name):
            return ctx.enter_context(nc.semaphore(name))

        ring = [ctx.enter_context(nc.psum_tensor(f"ring{k}", [P, HALF], F32)) for k in range(4)]
        rwb = ctx.enter_context(nc.psum_tensor("rwb", [P, HALF], F32))
        y = ctx.enter_context(nc.psum_tensor("y", [P, HALF], F32))
        tn = ctx.enter_context(nc.psum_tensor("tn", [P, HALF], F32))
        tp = ctx.enter_context(nc.psum_tensor("tp", [P, HALF], F32))

        w1_h, w1_l = sb("w1_h", [P, HW], F32R), sb("w1_l", [P, HW], F32R)
        w3_h, w3_l = sb("w3_h", [P, HW], F32R), sb("w3_l", [P, HW], F32R)
        w2_h, w2_l = sb("w2_h", [P, HW], F32R), sb("w2_l", [P, HW], F32R)
        WS = 2 * HID + D + 2 * D + E
        ws_h, ws_l = sb("ws_h", [P, WS], F32R), sb("ws_l", [P, WS], F32R)
        gw = sb("gw", [P, 2 * E], F32R)
        O_QK, O_OUT, O_GW = 2 * HID, 2 * HID + D, 2 * HID + 3 * D
        sel_sb = sb("sel_sb", [2 * E, P], F32R)
        b2_h, b2_lo = sb("b2_h", [3 * E, D], F32R), sb("b2_lo", [3 * E, D], F32R)
        bv_f = sb("bv_f", [2, HID])
        bv_h, bv_lo = sb("bv_h", [2, HID], F32R), sb("bv_lo", [2, HID], F32R)
        ones = sb("ones", [2, P], F32R)
        col = sb("col", [P, NCOL])
        hb2, warm = sb("hb2", [P, 1]), sb("warm", [P, 1])
        const = sb("const", [P, P + E * E + P])
        ident, margin = const[:, 0:P], const[:, P:P + E * E]
        ones_f = const[0:2, P + E * E:]

        xin, xa, xb = sb("xin", [P, KT * D]), sb("xa", [P, KT * D]), sb("xb", [P, KT * D])
        res = sb("res", [P, KT * D])
        st, mv = sb("st", [P, KT, 6]), sb("mv", [P, KT, 2])
        vv, ri, t1, t2 = sb("vv", [P, KT]), sb("ri", [P, KT], I32), sb("t1", [P, KT]), sb("t2", [P, KT])
        xn = sb("xn", [P, HALF])
        xt_h = [sb(f"xt_h{k}", [P, HALF], F32R) for k in range(2)]
        xt_l = [sb(f"xt_l{k}", [P, HALF], F32R) for k in range(2)]
        mx, sm, rc = sb("mx", [P, TT]), sb("sm", [P, TT]), sb("rc", [P, TT])
        lg, sl, dn, ex, sc, bi = (sb(k, [P, TT, E]) for k in ("lg", "sl", "dn", "ex", "sc", "bi"))
        diff, gt = sb("diff", [P, TT, E * E]), sb("gt", [P, TT, E * E])
        rank, rw = sb("rank", [P, TT, E]), sb("rw", [P, TT, E])
        rwh = sb("rwh", [P, TT, E], F32R)
        rw3 = sb("rw3", [P, TT, P])
        rwt = [sb(f"rwt{k}", [3 * E, HALF], F32R) for k in range(2)]
        u = [sb(f"u{k}", [P, HALF]) for k in range(2)]
        g = [sb(f"g{k}", [P, HALF]) for k in range(4)]
        p = [sb(f"p{k}", [P, HALF]) for k in range(2)]
        p_h = [sb(f"p_h{k}", [P, HALF], F32R) for k in range(4)]
        p_l = [sb(f"p_l{k}", [P, HALF], F32R) for k in range(4)]
        ys = sb("ys", [P, HALF])
        axf = sb("axf", [P, HALF])
        ax_h, ax_l = sb("ax_h", [P, N], F32R), sb("ax_l", [P, N], F32R)
        scratch = sb("scratch", [P, 6 * N])
        qkf, kqt = scratch[:, 0:N], scratch[:, N:2 * N]
        vf, gate = scratch[:, 2 * N:4 * N], scratch[:, 4 * N:6 * N]
        k_h, k_l = sb("k_h", [P, N], F32R), sb("k_l", [P, N], F32R)
        q_h, q_l = sb("q_h", [P, N], F32R), sb("q_l", [P, N], F32R)
        v_h, v_l = sb("v_h", [P, KT * HID], F32R), sb("v_l", [P, KT * HID], F32R)
        o_f, o_h, o_l = sb("o_f", [P, N]), sb("o_h", [P, N], F32R), sb("o_l", [P, N], F32R)

        w_loaded = [sem(f"w_loaded{k}") for k in range(7)]
        x_loaded = sem("x_loaded")
        stored = [sem(f"stored{k}") for k in range(2)]
        moved = sem("moved")
        gw_done = sem("gw_done")
        copies_done = sem("copies_done")
        setup_done = sem("setup_done")
        w_split = [sem(f"w_split{k}") for k in range(4)]
        passed_dve = sem("passed_dve")
        table_step = sem("table_step")
        norm_step, xn_ready, xt_done = sem("norm_step"), sem("xn_ready"), sem("xt_done")
        xh_done, xl_done = sem("xh_done"), sem("xl_done")
        lg_done, route_step, sl_done = sem("lg_done"), sem("route_step"), sem("sl_done")
        rt_done, rt_copied = sem("rt_done"), sem("rt_copied")
        w3_done, w1_done, rwb_done, w2_done = sem("w3_done"), sem("w1_done"), sem("rwb_done"), sem("w2_done")
        u_done, g_done, s_done, p_done = sem("u_done"), sem("g_done"), sem("s_done"), sem("p_done")
        hi_done, lo_done = sem("hi_done"), sem("lo_done")
        ys_done, yt_done, x1_done = sem("ys_done"), sem("yt_done"), sem("x1_done")
        axf_done, axh_done, axl_done = sem("axf_done"), sem("axh_done"), sem("axl_done")
        item_done, item_read = sem("item_done"), sem("item_read")
        kqf_done, kq_hi, kq_lo = sem("kqf_done"), sem("kq_hi"), sem("kq_lo")
        vh_done, vl_done = sem("vh_done"), sem("vl_done")
        a_done, ah_done, al_done, av_done = sem("a_done"), sem("ah_done"), sem("al_done"), sem("av_done")
        og_read, oh_done, o_split = sem("og_read"), sem("oh_done"), sem("o_split")
        z_done, zs_done, zt_done, x2_done = sem("z_done"), sem("zs_done"), sem("zt_done"), sem("x2_done")

        def c(k):
            return col[:, k:k + 1]

        def half(t, h):
            return t[:, h * HALF:(h + 1) * HALF]

        def tile(t, k):
            return t[:, k * P:(k + 1) * P]

        x_dram = x.rearrange("b (p t) d -> b p (t d)", p=P)
        out_dram = out.rearrange("b (p t) d -> b p (t d)", p=P)
        sel_f, b2_f = res[0:2 * E, 0:P], res[0:3 * E, HALF:HALF + D]
        stage = [scratch[:, k * HW:(k + 1) * HW] for k in range(3)]
        acc = [y, tp]
        zbank = [rwb, tp]

        block = ctx.enter_context(nc.Block())

        @block.sync
        def _(sp):
            sp.dma_start(xin[:], x_dram[0]).then_inc(x_loaded, 16)
            sp.dma_start(col[:], cols).then_inc(w_loaded[1], 16)
            sp.dma_start(xb[:, 0:WS], wsmall).then_inc(w_loaded[2], 16)
            sp.dma_start(const[:], consts).then_inc(w_loaded[0], 16)
            sp.dma_start(stage[1], w3).then_inc(w_loaded[3], 16)
            sp.dma_start(stage[0], w1).then_inc(w_loaded[4], 16)
            sp.dma_start(stage[2], w2).then_inc(w_loaded[5], 16)
            sp.dma_start(sel_f, sel).then_inc(stored[0], 16)
            sp.dma_start(b2_f, b2).then_inc(stored[1], 16)
            for k in range(2):
                sp.dma_start(bv_f[k:k + 1, :], bv).then_inc(w_loaded[6], 16)
            sp.wait_ge(setup_done, SETUP)
            sp.dma_start(b2_h[2 * E:, :].bitcast(F32), b2_lo[2 * E:, :].bitcast(F32)).then_inc(moved, 16)
            sp.dma_start(bv_h[1:2, :].bitcast(F32), bv_lo[1:2, :].bitcast(F32)).then_inc(moved, 16)
            sp.wait_ge(x1_done, 2)
            sp.dma_start(xin[:], x_dram[1]).then_inc(x_loaded, 16)

            def turn(t, batch, following):
                sp.wait_ge(x1_done, (Count(4, 4, t)).value)
                sp.dma_start(xin[:], x_dram[following]).then_inc(x_loaded, 16)
                for h in range(2):
                    sp.wait_ge(x1_done, (Count(5 + h, 4, t)).value)
                    sp.dma_start(half(out_dram[batch], h), half(res, h)).then_inc(stored[h], 16)

            with sp.Fori(0, B - 2) as t:
                turn(t, t, t + 2)
            last = 4 * (B - 2)
            sp.wait_ge(x1_done, last + 4)
            sp.dma_start(xin[:], x_dram[0]).then_inc(x_loaded, 16)
            for h in range(2):
                sp.wait_ge(x1_done, last + 5 + h)
                sp.dma_start(half(out_dram[B - 2], h), half(res, h)).then_inc(stored[h], 16)
            for h in range(2):
                sp.wait_ge(x1_done, 4 * B - 1 + h)
                sp.dma_start(half(out_dram[B - 1], h), half(res, h)).then_inc(stored[h], 16)
            sp.wait_ge(x_loaded, 16 * (B + 1))
            for h in range(2):
                sp.wait_ge(stored[h], 16 * (B + 1))

        @block.tensor
        def _(pe):
            mm = nc.tensor.matmul

            def product(out, a_h, a_l, b_h, b_l, start=True, stop=True):
                mm(out, a_h, b_h, start=start, stop=False)
                mm(out, a_l, b_h, start=False, stop=False)
                return mm(out, a_h, b_l, start=False, stop=stop)

            def turn_x(n, h=0):
                pe.wait_ge(xn_ready, (n.i + h + 1).value)
                if h == 1:
                    pe.wait_ge(axf_done, (n.b * 2 + 1).value)
                elif n.before_kind == "ffn":
                    pe.wait_ge(rt_copied, n.before.value)
                elif n.before_kind == "att":
                    pe.wait_ge(axf_done, n.before.value)
                for k in range(TT):
                    last = nc.tensor.transpose(tile(tn, k), tile(xn, k), ident)
                last.then_inc(xt_done, 1)

            def logits(n):
                pe.wait_ge(xl_done, (n.r + 1).value)
                xh, xl = xt_h[n.r.mod(2)], xt_l[n.r.mod(2)]
                for k in range(TT):
                    out = tn[:, 2 * k * E:2 * (k + 1) * E]
                    mm(out, tile(xh, k), gw[:], start=True, stop=False)
                    last = mm(out, tile(xl, k), gw[:], start=False, stop=True)
                last.then_inc(lg_done, 1)

            def turn_route(n):
                pe.wait_ge(table_step, (n.table * TABLE_STEPS + TABLE_STEPS).value)
                for k in range(TT):
                    last = nc.tensor.transpose(tile(tn, k), rw3[:, k, :], ident)
                last.then_inc(rt_done, 1)

            def down(ch, j):
                n = ch.q * NBL + j
                rt = rwt[ch.r.mod(2)]
                if j == 0:
                    mm(y[:], b2_h[:], rt[:], start=True, stop=False)
                pe.wait_ge(lo_done, (n + 1).value)
                product(y[:], tile(w2_h, j), tile(w2_l, j), p_h[n.mod(4)][:], p_l[n.mod(4)][:],
                        start=False, stop=(j == NBL - 1)).then_inc(w2_done, 1)

            def spread_weights(ch, before):
                pe.wait_ge(rt_copied, (ch.q + 1).value)
                if before is None:
                    pe.wait_ge(setup_done, 4)
                if before == "att":
                    pe.wait_ge(x2_done, (ch.att_b * 2 + 1).value)
                if (ch.q * NR).due:
                    pe.wait_ge(p_done, (ch.q * NR).value)
                mm(rwb[:], sel_sb[:], rwt[ch.r.mod(2)][0:2 * E, :], start=True, stop=True).then_inc(rwb_done, 1)

            def turn_y(ch):
                pe.wait_ge(ys_done, (ch.q + 1).value)
                if ch.q.due:
                    pe.wait_ge(x1_done, ch.q.value)
                for k in range(TT):
                    last = nc.tensor.transpose(tile(tp, k), tile(ys, k), ident)
                last.then_inc(yt_done, 1)

            def scores(b, m):
                h, j = divmod(m, KT)
                item = score_item(m)
                if m in (0, KT // 2, KT):
                    pe.wait_ge(kq_lo, (b * 4 + {0: 2, KT // 2: 3, KT: 4}[m]).value)
                pe.wait_ge(item_read, (b * RING + read_before(item)).value)
                product(ring[bank_of(item)][:], tile(k_h, j), tile(k_l, j), half(q_h, h), half(q_l, h))\
                    .then_inc(item_done, 1)

            def gate_product(b, k):
                hb, h = divmod(k, 2)
                item = gate_item(k)
                pe.wait_ge(item_read, (b * RING + read_before(item)).value)
                w = slice(HID + hb * P, HID + (hb + 1) * P)
                product(ring[bank_of(item)][:], ws_h[:, w], ws_l[:, w], half(ax_h, h), half(ax_l, h))\
                    .then_inc(item_done, 1)

            def values(b, m):
                h, j = divmod(m, KT)
                if h == 0 and j % 2 == 0:
                    pe.wait_ge(vl_done, (b * TT + j // 2 + 1).value)
                pe.wait_ge(al_done, (b * (2 * KT) + m + 1).value)
                for k in range(2):
                    if m == KT:
                        pe.wait_ge(og_read, (b * 4 + k + 1).value)
                    cut = slice(j * HID + k * P, j * HID + (k + 1) * P)
                    last = product(acc[k][:], v_h[:, cut], v_l[:, cut], p_h[(m + 1) % 4][:], p_l[(m + 1) % 4][:],
                                   start=(j == 0), stop=(j == KT - 1))
                last.then_inc(av_done, 1)

            def project(b, h):
                for k in range(2):
                    pe.wait_ge(o_split, (b * 4 + 2 * h + k + 1).value)
                    w = slice(O_OUT + k * D, O_OUT + (k + 1) * D)
                    last = product(zbank[h][:], ws_h[:, w], ws_l[:, w], half(o_h, k), half(o_l, k),
                                   start=(k == 0), stop=(k == 1))
                last.then_inc(z_done, 1)

            def turn_z(b, h):
                pe.wait_ge(zs_done, (b * 2 + h + 1).value)
                for k in range(TT):
                    last = nc.tensor.transpose(tile(zbank[h], k), tile(ys, k), ident)
                last.then_inc(zt_done, 1)

            def ffn(ch, before, pending, prep, att=None, following=None):
                xh, xl = xt_h[ch.r.mod(2)], xt_l[ch.r.mod(2)]
                att_b = None if before != "att" else ch.att_b
                pe.wait_ge(xl_done, (ch.r + 1).value)
                for j in range(NBL):
                    n = ch.q * NBL + j
                    if j < 2 and before == "att":
                        pe.wait_ge(item_read, (att_b * RING + RING - 2 + 2 * j).value)
                    elif j < 2 and before is None:
                        pass
                    else:
                        pe.wait_ge(g_done, (n - 1).value)
                    pair = 2 * n.mod(2)
                    if before is None and j in (0, PIECE):
                        pe.wait_ge(w_split[1], 1 + j // PIECE)
                    product(ring[pair][:], tile(w3_h, j), tile(w3_l, j), xh[:], xl[:]).then_inc(w3_done, 1)
                    if prep and j == (6 if prep.kind == "ffn" else 5):
                        turn_x(prep)
                    if prep and prep.kind == "att" and j == 8:
                        turn_x(prep, 1)
                    if before is None and j in (0, PIECE):
                        pe.wait_ge(w_split[2], 1 + j // PIECE)
                    product(ring[pair + 1][:], tile(w1_h, j), tile(w1_l, j), xh[:], xl[:]).then_inc(w1_done, 1)
                    if j == 1:
                        spread_weights(ch, before)
                    if j >= LAG:
                        if j == LAG and before == "ffn":
                            pe.wait_ge(ys_done, ch.q.value)
                        if j == LAG and before == "att":
                            pe.wait_ge(og_read, (att_b * 4 + 3).value)
                        if before is None and j == LAG:
                            pe.wait_ge(w_split[3], 1)
                            pe.wait_ge(moved, 32)
                        down(ch, j - LAG)
                    elif pending and before == "ffn":
                        down(ch.before, NBL - LAG + j)
                    elif pending and before == "att":
                        values(att_b, 2 * KT - LAG + j)
                    if j == 0:
                        turn_route(ch.norm)
                    if pending and before == "ffn" and j == 3:
                        turn_y(ch.before)
                    if pending and before == "att" and j == 8:
                        project(att_b, 1)
                    if pending and before == "att" and j == 10:
                        turn_z(att_b, 1)
                    if prep and prep.kind == "ffn" and j == 7:
                        logits(prep)

            def ffn_rest(ch):
                for j in range(NBL - LAG, NBL):
                    down(ch, j)
                turn_y(ch)

            def attention(b, last_chunk, pending, prep):
                q = last_chunk.q
                for h in range(2):
                    pe.wait_ge(axl_done, (b * 2 + h + 1).value)
                    if h == 0:
                        pe.wait_ge(g_done, (q * NBL + NBL - 1).value)
                    product(ring[h][:], ws_h[:, O_QK:O_QK + D], ws_l[:, O_QK:O_QK + D],
                            half(ax_h, h), half(ax_l, h)).then_inc(item_done, 1)
                if pending:
                    down(last_chunk, NBL - 3)
                pe.wait_ge(g_done, (q * NBL + NBL).value)
                for k in range(TT):
                    item = 2 + k
                    if item >= 4:
                        pe.wait_ge(item_read, (b * RING + item - 3).value)
                    for t in range(2):
                        o = ring[bank_of(item)][:, t * HID:(t + 1) * HID]
                        xs = 2 * k + t
                        mm(o, tile(ax_h, xs), ws_h[:, 0:HID], start=True, stop=False)
                        mm(o, tile(ax_l, xs), ws_h[:, 0:HID], start=False, stop=False)
                        mm(o, tile(ax_h, xs), ws_l[:, 0:HID], start=False, stop=False)
                        last = mm(o, ones[:], bv_h[:], start=False, stop=True)
                    last.then_inc(item_done, 1)
                    if pending and k == 1:
                        down(last_chunk, NBL - 2)
                    if pending and k == 3:
                        down(last_chunk, NBL - 1)
                for m in range(2 * KT):
                    if m < 4:
                        gate_product(b, m)
                    if m != 12:
                        scores(b, m)
                    if m == 11:
                        scores(b, m + 1)
                    if pending and m == 0:
                        turn_y(last_chunk)
                    if m == LAG:
                        pe.wait_ge(x1_done, (q + 1).value)
                    if m >= LAG:
                        values(b, m - LAG)
                    if m == 3:
                        turn_x(prep)
                    if m == 5:
                        logits(prep)
                    if m == 14:
                        project(b, 0)
                    if m == 15:
                        turn_z(b, 0)

            def attention_rest(b, first):
                for m in range(2 * KT - LAG, 2 * KT):
                    values(b, m)
                turn_x(first)
                logits(first)
                project(b, 1)
                turn_z(b, 1)

            def start(first):
                pe.wait_ge(w_loaded[0], 16)
                turn_x(first)
                pe.wait_ge(gw_done, 1)
                pe.wait_ge(w_split[0], 1)
                logits(first)

            link_chunks_and_run(
                pe, ffn, ffn_rest, attention, attention_rest,
                prepare_att=lambda n, following: (turn_x(n), turn_x(n, 1)),
                start=start,
            )

        @block.scalar
        def _(act):
            act_fn = nc.scalar.activation

            def copy_x(n, h=0):
                act.wait_ge(xt_done, (n.i + h + 1).value)
                if n.kind == "ffn":
                    if (n.q * NBL).due:
                        act.wait_ge(w1_done, (n.q * NBL).value)
                    act_fn(xt_h[n.r.mod(2)][:], tn[:], ACT.Copy).then_inc(xh_done, 1)
                else:
                    if (n.b * 2 + h).due:
                        act.wait_ge(axl_done, (n.b * 2 + h).value)
                    act_fn(axf[:], tn[:], ACT.Identity, bias=c(C_LNB), scale=c(C_LNS)).then_inc(axf_done, 1)

            def silu_logits(n):
                act.wait_ge(route_step, (n.r * ROUTE_STEPS + 3).value)
                act_fn(sl[:], lg[:], ACT.Silu).then_inc(sl_done, 1)

            def copy_route(n):
                act.wait_ge(rt_done, (n.table + 1).value)
                if (n.q * NBL).due:
                    act.wait_ge(w2_done, (n.q * NBL).value)
                act_fn(rwt[n.r.mod(2)][:], tn[0:3 * E, :], ACT.Copy).then_inc(rt_copied, 1)

            def up(ch, j, before):
                n = ch.q * NBL + j
                act.wait_ge(w3_done, (n + 1).value)
                if j < 2 and before == "att":
                    act.wait_ge(a_done, (ch.att_b * (2 * KT) + 2 * KT - 1 + j).value)
                else:
                    if (n - 1).due:
                        act.wait_ge(g_done, (n - 1).value)
                act_fn(u[n.mod(2)][:], ring[2 * n.mod(2)][:], ACT.Identity, bias=c(C_B3 + j))\
                    .then_inc(u_done, 1)

            def silu(ch, j):
                n = ch.q * NBL + j
                act.wait_ge(g_done, (n + 1).value)
                if j < NR:
                    act_fn(g[n.mod(4)][:], g[n.mod(4)][:], ACT.Silu).then_inc(s_done, 1)
                else:
                    act.wait_ge(lo_done, (n - 1).value)
                    act_fn(p[n.mod(2)][:], g[n.mod(4)][:], ACT.Silu).then_inc(s_done, 1)

            def high(ch, j, before=None):
                n = ch.q * NBL + j
                if j < NR:
                    act.wait_ge(p_done, (ch.q * NR + j + 1).value)
                else:
                    act.wait_ge(s_done, (n + 1).value)
                if j < 4 and before == "att":
                    act.wait_ge(av_done, (ch.att_b * (2 * KT) + min(2 * KT - 2 + j, 2 * KT)).value)
                else:
                    if (n - 3).due:
                        act.wait_ge(w2_done, (n - 3).value)
                act_fn(p_h[n.mod(4)][:], p[n.mod(2)][:], ACT.Copy).then_inc(hi_done, 1)

            def half_y(ch):
                act.wait_ge(w2_done, (ch.q * NBL + NBL).value)
                if ch.q.due:
                    act.wait_ge(yt_done, ch.q.value)
                act_fn(ys[:], y[:], ACT.Identity, bias=hb2[:, 0:1], scale=0.5).then_inc(ys_done, 1)

            def ffn(ch, before, pending, prep, att=None, following=None):
                for j in range(NBL):
                    if prep and prep.kind == "ffn" and j == 9:
                        silu_logits(prep)
                    if j >= 1:
                        silu(ch, j - 1)
                    up(ch, j, before)
                    if pending and before == "ffn" and j == 0:
                        silu(ch.before, NBL - 1)
                    if prep and j == (6 if prep.kind == "ffn" else 5):
                        copy_x(prep)
                    if prep and prep.kind == "att" and j == 8:
                        copy_x(prep, 1)
                    if pending and before == "ffn" and j == 2:
                        half_y(ch.before)
                    if j == 0:
                        copy_route(ch.norm)
                    if j >= 1:
                        high(ch, j - 1, before)
                    elif pending and before == "ffn":
                        high(ch.before, NBL - 1)
                    if pending and before == "att" and j == 9:
                        bias_z(ch.att_b, 1)

            def ffn_rest(ch):
                silu(ch, NBL - 1)
                high(ch, NBL - 1)
                half_y(ch)

            def bias_z(b, h):
                act.wait_ge(z_done, (b * 2 + h + 1).value)
                if h == 0:
                    act.wait_ge(yt_done, (ys_uses_before(b)).value)
                else:
                    act.wait_ge(zt_done, (b * 2 + 1).value)
                act_fn(ys[:], zbank[h][:], ACT.Identity, bias=c(C_BO)).then_inc(zs_done, 1)

            def item(b, k):
                act.wait_ge(item_done, (b * RING + k + 1).value)
                bank = ring[bank_of(k)]
                if k < 2:
                    if (b * 4).due:
                        act.wait_ge(kqf_done, (b * 4).value)
                    act_fn(half(qkf, k), bank[:], ACT.Silu, bias=c(C_BQK)).then_inc(item_read, 1)
                elif k < 2 + TT:
                    if (b * TT + k - 2 - TT + 1).due:
                        act.wait_ge(vl_done, (b * TT + k - 2 - TT + 1).value)
                    act_fn(half(vf, k - 2), bank[:], ACT.Silu).then_inc(item_read, 1)
                else:
                    kk = (k - SIM0) // 2
                    if (b * 4).due:
                        act.wait_ge(og_read, (b * 4).value)
                    act_fn(gate[:, kk * HALF:(kk + 1) * HALF], bank[:], ACT.Silu,
                           bias=c(C_BG + kk // 2)).then_inc(item_read, 1)

            def relu(b, m):
                act.wait_ge(item_done, (b * RING + score_item(m) + 1).value)
                if m < 2:
                    act.wait_ge(g_done, (after_ffn(b)).value)
                else:
                    act.wait_ge(a_done, (b * (2 * KT) + m - 1).value)
                act_fn(u[m % 2][:], ring[bank_of(score_item(m))][:], ACT.Relu, scale=1.0 / N).then_inc(item_read, 1)

            def attention(b, last_chunk, pending, prep):
                if pending:
                    silu(last_chunk, NBL - 1)
                item(b, 0)
                if pending:
                    high(last_chunk, NBL - 1)
                item(b, 1)
                for k in range(2, 2 + TT):
                    item(b, k)
                if pending:
                    half_y(last_chunk)
                for m in range(2 * KT):
                    if m == 15:
                        bias_z(b, 0)
                    if m < 4:
                        item(b, gate_item(m))
                    relu(b, m)
                    if m == 3:
                        copy_x(prep)
                    if m == 7:
                        silu_logits(prep)

            def attention_rest(b, first):
                copy_x(first)
                silu_logits(first)
                bias_z(b, 1)

            def high_weight(k, dst, src, cut=slice(0, None)):
                act.wait_ge(w_loaded[2 + k], 16)
                act_fn(dst[:, cut], src[:, cut], ACT.Copy).then_inc(copies_done, 1)

            def start(first):
                act.wait_ge(w_loaded[1], 16)
                act_fn(warm[:], c(0), ACT.Silu)
                high_weight(0, ws_h, xb[:, 0:WS])
                act_fn(gw[:, 0:E], xb[:, O_GW:WS], ACT.Copy).then_inc(gw_done, 1)
                high_weight(1, w3_h, stage[1], FIRST)
                copy_x(first)
                high_weight(2, w1_h, stage[0], FIRST)
                high_weight(1, w3_h, stage[1], REST)
                silu_logits(first)
                high_weight(2, w1_h, stage[0], REST)
                high_weight(3, w2_h, stage[2])
                act.wait_ge(setup_done, 3)

            link_chunks_and_run(
                act, ffn, ffn_rest, attention, attention_rest,
                prepare_att=lambda n, following: (copy_x(n), copy_x(n, 1)),
                start=start,
            )

        @block.vector
        def _(dve):
            v = nc.vector

            def sources(n):
                return {"xin": xin, "xa": xa, "xb": xb}[n.source]

            def norm(n, part):
                at = n.u * NORM_STEPS
                src = sources(n)
                tiles = TT * len(n.halves)
                if n.kind == "ffn":
                    src = half(src, n.half)
                if part == 0:
                    if at.due:
                        dve.wait_ge(norm_step, at.value)
                    if n.source == "xin" and n.half == 0:
                        dve.wait_ge(x_loaded, ((n.b + 1) * 16).value)
                    if n.source == "xa":
                        dve.wait_ge(x1_done, n.q_of_source.value)
                    if n.source == "xb":
                        dve.wait_ge(x2_done, (n.b * 2 + n.half + 1).value)
                    for k in range(TT):
                        last = v.bn_stats(st[:, k, :], tile(src, k))
                    if n.kind == "ffn":
                        last.then_inc(norm_step, 1)
                elif part == "second":
                    dve.wait_ge(x1_done, (n.q_of_source + 1).value)
                    for k in range(TT, tiles):
                        last = v.bn_stats(st[:, k, :], tile(src, k))
                    last.then_inc(norm_step, 1)
                elif part == 1:
                    if n.i.due:
                        dve.wait_ge(xn_ready, n.i.value)
                    dve.wait_ge(norm_step, (at + 1).value)
                    dve.sem_inc(passed_dve, 1)
                    for k in range(tiles):
                        last = v.bn_aggr(mv[:, k, :], st[:, k, :])
                    last.then_inc(norm_step, 1)
                else:
                    h = part - 2
                    dve.wait_ge(norm_step, (at + NORM_STEPS).value)
                    if (n.i + h).due:
                        dve.wait_ge(xt_done, (n.i + h).value)
                    for k in range(TT):
                        t = h * TT + k
                        last = v.tensor_scalar(tile(xn, k), tile(src, t), mv[:, t, 0:1],
                                               ri[:, t:t + 1].bitcast(F32), ALU.subtract, ALU.mult)
                    last.then_inc(xn_ready, 1)

            def newton(n, *steps):
                tiles = TT * len(n.halves)
                vt, rt_, t1_, t2_ = vv[:, 0:tiles], ri[:, 0:tiles], t1[:, 0:tiles], t2[:, 0:tiles]
                r = rt_.bitcast(F32)
                one, two = (1.0, EPS) if n.kind == "ffn" else (1.0 + EPS, EPS * EPS)
                for k in steps:
                    dve.wait_ge(norm_step, (n.u * NORM_STEPS + 2 + k).value)
                    if k == 0:
                        last = v.tensor_scalar(vt, mv[:, 0:tiles, 1], one, two, ALU.mult, ALU.add)
                    elif k == 1:
                        last = v.tensor_scalar(rt_, vt.bitcast(I32), 1, None, ALU.logical_shift_right)
                    elif k == 2:
                        last = v.tensor_scalar(rt_, rt_, -1.0, float(0x5F3759DF), ALU.mult, ALU.add)
                    elif k % 3 == 0:
                        last = v.scalar_tensor_tensor(t1_, r, -0.5, r, ALU.mult, ALU.mult)
                    elif k % 3 == 1:
                        last = v.tensor_tensor(t2_, t1_, vt, ALU.mult)
                    else:
                        last = v.scalar_tensor_tensor(r, t2_, 1.5, r, ALU.add, ALU.mult)
                    last.then_inc(norm_step, 1)

            def low_x(n):
                dve.wait_ge(xh_done, (n.r + 1).value)
                k = n.r.mod(2)
                v.tensor_tensor(xt_l[k][:], tn[:], xt_h[k][:].bitcast(F32), ALU.subtract).then_inc(xl_done, 1)

            def high_ax(n, h):
                dve.wait_ge(axf_done, (n.b * 2 + h + 1).value)
                v.tensor_copy(half(ax_h, h), axf[:]).then_inc(axh_done, 1)

            def wide(t):
                return t[:].unsqueeze(2).to_broadcast([P, TT, E])

            def route(n, *steps):
                made = n.table * TABLE_STEPS if n.table is not None else None
                for k in steps:
                    if k < ROUTE_STEPS:
                        if (n.r * ROUTE_STEPS + k).due:
                            dve.wait_ge(route_step, (n.r * ROUTE_STEPS + k).value)
                    elif k == ROUTE_STEPS:
                        dve.wait_ge(route_step, ((n.r + 1) * ROUTE_STEPS).value)
                    if k == 0:
                        both = tn[:, 0:2 * TT * E].rearrange("p (t k e) -> p t e k", k=2, e=E)
                        dve.wait_ge(lg_done, (n.r + 1).value)
                        last = v.tensor_reduce(dn[:], both, AX.X, ALU.add)
                    elif k == 1:
                        last = v.tensor_reduce(mx[:], dn[:], AX.X, ALU.max)
                    elif k == 2:
                        last = v.tensor_tensor(lg[:], dn[:], wide(mx), ALU.subtract)
                    elif k == 3:
                        dve.wait_ge(sl_done, (n.r + 1).value)
                        last = v.scalar_tensor_tensor(dn[:], lg[:], TINY, sl[:], ALU.subtract, ALU.subtract)
                    elif k == 4:
                        last = v.reciprocal(dn[:], dn[:])
                    elif k == 5:
                        last = v.scalar_tensor_tensor(ex[:], sl[:], TINY, dn[:], ALU.subtract, ALU.mult)
                    elif k == 6:
                        last = v.tensor_reduce(sm[:], ex[:], AX.X, ALU.add)
                    elif k == 7:
                        last = v.reciprocal(rc[:], sm[:])
                    elif k == 8:
                        last = v.tensor_tensor(sc[:], ex[:], wide(rc), ALU.mult)
                    elif k == 9:
                        gb = col[:, C_GB:C_GB + E].unsqueeze(1).to_broadcast([P, TT, E])
                        last = v.tensor_tensor(bi[:], sc[:], gb, ALU.add)
                    elif k == 10:
                        mine = bi[:].unsqueeze(3).to_broadcast([P, TT, E, E])
                        other = bi[:].unsqueeze(2).to_broadcast([P, TT, E, E])
                        last = v.tensor_tensor(diff[:].rearrange("p t (e f) -> p t e f", f=E), other, mine,
                                               ALU.subtract)
                    elif k == 11:
                        least = margin.unsqueeze(1).to_broadcast([P, TT, E * E])
                        last = v.tensor_tensor(gt[:], diff[:], least, ALU.is_ge)
                    elif k == 12:
                        last = v.tensor_reduce(rank[:], gt[:].rearrange("p t (e f) -> p t e f", f=E), AX.X, ALU.add)
                    elif k == 13:
                        if made.due:
                            dve.wait_ge(table_step, made.value)
                        last = v.scalar_tensor_tensor(rw[:], rank[:], 2.0, sc[:], ALU.is_lt, ALU.mult)
                    elif k == 14:
                        dve.wait_ge(table_step, (made + 1).value)
                        last = v.tensor_copy(rwh[:], rw[:])
                    else:
                        dve.wait_ge(table_step, (made + 2).value)
                        if n.table.due:
                            dve.wait_ge(rt_done, n.table.value)
                        high = rwh[:].bitcast(F32).unsqueeze(2).to_broadcast([P, TT, 2, E])
                        v.tensor_copy(rw3[:, :, 0:4 * E].rearrange("p t (k e) -> p t k e", e=2 * E)[:, :, :, 0:E],
                                      high).then_inc(table_step, 1)
                        last = v.tensor_tensor(rw3[:, :, E:2 * E], rw[:], rwh[:].bitcast(F32), ALU.subtract)
                    last.then_inc(route_step if k < ROUTE_STEPS else table_step, 1)

            def product(ch, j, before):
                n = ch.q * NBL + j
                dve.wait_ge(w1_done, (n + 1).value)
                dve.wait_ge(u_done, (n + 1).value)
                if j < 4 and before == "att":
                    dve.wait_ge(al_done, (ch.att_b * (2 * KT) + min(2 * KT - 2 + j, 2 * KT)).value)
                else:
                    if (n - 3).due:
                        dve.wait_ge(s_done, (n - 3).value)
                    done = ch.q * NR + max(j - 3, 0)
                    if done.due:
                        dve.wait_ge(p_done, done.value)
                v.scalar_tensor_tensor(g[n.mod(4)][:], ring[2 * n.mod(2) + 1][:], c(C_B1 + j), u[n.mod(2)][:],
                                       ALU.add, ALU.mult).then_inc(g_done, 1)

            def weigh(ch, j):
                n = ch.q * NBL + j
                dve.wait_ge(s_done, (n + 1).value)
                dve.wait_ge(rwb_done, (ch.q + 1).value)
                if (n - 1).due:
                    dve.wait_ge(lo_done, (n - 1).value)
                v.tensor_tensor(p[n.mod(2)][:], g[n.mod(4)][:], rwb[:], ALU.mult).then_inc(p_done, 1)

            def residual(ch):
                dve.wait_ge(yt_done, (ch.q + 1).value)
                src, dst = (xin, xa) if ch.ffn == 1 else (xb, res)
                if ch.ffn == 2:
                    dve.wait_ge(stored[ch.half], (ch.b * 16 + 16).value)
                else:
                    if (ch.b * 2 + ch.half - 1).due:
                        dve.wait_ge(x2_done, (ch.b * 2 + ch.half - 1).value)
                v.tensor_tensor(half(dst, ch.half), half(src, ch.half), tp[:], ALU.add).then_inc(x1_done, 1)

            def gate_o(b, h, part):
                dve.wait_ge(av_done, (b * (2 * KT) + (h + 1) * KT).value)
                dve.wait_ge(item_read, (b * RING + gate_item(3) + 1).value)
                if (b * 4 + 2 * h).due:
                    dve.wait_ge(o_split, (b * 4 + 2 * h).value)
                v.tensor_tensor(half(o_f, part), acc[part][:],
                                gate[:, (2 * part + h) * HALF:(2 * part + h + 1) * HALF], ALU.mult).then_inc(og_read, 1)

            def split_o(b, h, part):
                if part == 0:
                    dve.wait_ge(og_read, (b * 4 + 2 * h + 2).value)
                    if (b * 2 + h).due:
                        dve.wait_ge(z_done, (b * 2 + h).value)
                    v.tensor_copy(o_h[:], o_f[:]).then_inc(oh_done, 1)
                else:
                    dve.wait_ge(oh_done, (b * 2 + h + 1).value)
                    for k in range(2):
                        v.tensor_tensor(half(o_l, k), half(o_f, k), half(o_h, k).bitcast(F32), ALU.subtract)\
                            .then_inc(o_split, 1)

            def residual_z(b, h):
                dve.wait_ge(zt_done, (b * 2 + h + 1).value)
                dve.wait_ge(x1_done, (b * 4 + h + 1).value)
                v.tensor_tensor(half(xb, h), half(xa, h), zbank[h][:], ALU.add).then_inc(x2_done, 1)

            def ffn(ch, before, pending, prep, att=None, following=None):
                def sides(j, spot):
                    if prep is None:
                        return
                    if prep.kind == "ffn":
                        newton(prep, *{(1, 2): (0, 1, 2), (2, 0): (3,), (2, 1): (4,), (2, 2): (5,), (3, 0): (6,),
                                       (3, 1): (7,), (3, 2): (8, 9), (4, 0): (10,), (4, 1): (11,)}.get((j, spot), ()))
                        route(prep, *{(8, 1): (0,), (8, 2): (1, 2), (9, 1): (3,), (9, 2): (4,), (10, 0): (5,),
                                      (10, 1): (6,), (10, 2): (7, 8), (11, 0): (9,), (11, 1): (10,), (11, 2): (11,),
                                      (12, 0): (12, 13, 14, 15)}.get((j, spot), ()))
                        return
                    newton(prep, *{(0, 2): (0, 1, 2), (1, 0): (3,), (1, 1): (4,), (1, 2): (5,), (2, 0): (6,),
                                   (2, 1): (7,), (2, 2): (8,), (3, 0): (9,), (3, 1): (10,), (3, 2): (11,)}
                           .get((j, spot), ()))
                    if (j, spot) == (8, 2):
                        norm(following, 1)
                    newton(following, *{(9, 0): (0,), (9, 1): (1,), (10, 0): (2,), (10, 1): (3,), (10, 2): (4,), (11, 0): (5,),
                                        (11, 1): (6,), (11, 2): (7,), (12, 0): (8,), (12, 1): (9,), (12, 2): (10, 11)}
                           .get((j, spot), ()))

                for j in range(NBL):
                    if j == 0 and ch.norm.after_att:
                        route(ch.norm, 13, 14)
                        if pending:
                            residual_z(ch.att_b, 0)
                        route(ch.norm, 15)
                    if pending and before == "att" and j == 3:
                        gate_o(ch.att_b, 1, 0)
                    sides(j, 0)
                    if 1 <= j <= NR:
                        weigh(ch, j - 1)
                    sides(j, 1)
                    product(ch, j, before)
                    if pending and before == "ffn" and j == 5:
                        residual(ch.before)
                    if pending and before == "att":
                        if j == 3:
                            gate_o(ch.att_b, 1, 1)
                        if j == 5:
                            split_o(ch.att_b, 1, 0)
                        if j == 11:
                            residual_z(ch.att_b, 1)
                    if prep and prep.kind == "ffn" and j < 2:
                        norm(prep, j)
                    if prep and prep.kind == "att" and j == 0:
                        norm(prep, 1)
                    sides(j, 2)
                    if prep and prep.kind == "ffn":
                        if j == 4:
                            norm(prep, 2)
                        if j == 6:
                            low_x(prep)
                    if att and j == 7:
                        norm(att, 0)
                    if att and prep and j == 8:
                        norm(att, "second")
                    if prep and prep.kind == "att":
                        if j in (3, 6):
                            norm(prep, 1 + j // 3)
                        if j in (5, 9):
                            high_ax(prep, j // 9)
                        if j == 7:
                            norm(following, 0)

            def kq(b, k):
                dve.wait_ge(item_read, (b * RING + k // 2 + 1).value)
                if (b * 4 + k - 1).due:
                    dve.wait_ge(kq_lo, (b * 4 + k - 1).value)
                w, bb = (C_KW, C_KB) if k % 2 == 0 else (C_QW, C_QB)
                v.tensor_scalar(half(kqt, k % 2), half(qkf, k // 2), c(w), c(bb), ALU.mult, ALU.add)\
                    .then_inc(kqf_done, 1)
                dve.wait_ge(kqf_done, (b * 4 + k + 1).value)
                v.tensor_copy(half((k_h, q_h)[k % 2], k // 2), half(kqt, k % 2)).then_inc(kq_hi, 1)

            def split_v(b, k):
                cut = slice(k * HALF, (k + 1) * HALF)
                dve.wait_ge(item_read, (b * RING + 2 + k + 1).value)
                v.tensor_copy(v_h[:, cut], half(vf, k)).then_inc(vh_done, 1)
                dve.wait_ge(vh_done, (b * TT + k + 1).value)
                v.tensor_tensor(v_l[:, cut], half(vf, k), v_h[:, cut].bitcast(F32), ALU.subtract)\
                    .then_inc(vl_done, 1)

            def square(b, m):
                dve.wait_ge(item_read, (b * RING + score_item(m) + 1).value)
                if m == 0:
                    dve.wait_ge(s_done, (after_ffn(b)).value)
                    dve.wait_ge(w2_done, (after_ffn(b)).value)
                    dve.wait_ge(p_done, (b * (4 * NR) + 2 * NR).value)
                if m >= 4:
                    dve.wait_ge(al_done, (b * (2 * KT) + m - 3).value)
                v.tensor_tensor(g[(m + 1) % 4][:], u[m % 2][:], u[m % 2][:], ALU.mult).then_inc(a_done, 1)
                dve.wait_ge(a_done, (b * (2 * KT) + m + 1).value)
                if m >= 4:
                    dve.wait_ge(av_done, (b * (2 * KT) + m - 3).value)
                v.tensor_copy(p_h[(m + 1) % 4][:], g[(m + 1) % 4][:]).then_inc(ah_done, 1)

            def attention(b, last_chunk, pending, prep):
                kq(b, 0)
                kq(b, 1)
                for k in range(TT):
                    split_v(b, k)
                kq(b, 2)
                for m in range(2 * KT):
                    if m == 10:
                        gate_o(b, 0, 0)
                        gate_o(b, 0, 1)
                    if m == 2:
                        norm(prep, 2)
                    square(b, m)
                    if m == 3:
                        kq(b, 3)
                    if pending and m == 1:
                        residual(last_chunk)
                    if m == 4:
                        low_x(prep)
                    if 6 <= m <= 8:
                        route(prep, *((0, 1, 2), (3, 4, 5), (6, 7, 8, 9))[m - 6])
                    if m in (11, 12):
                        split_o(b, 0, m - 11)
                    if m in (13, 14):
                        route(prep, *((10, 11), (12,))[m - 13])

            def attention_rest(b, first):
                residual_z(b, 0)
                norm(first, 0)
                norm(first, 1)
                newton(first, *range(12))
                norm(first, 2)
                gate_o(b, 1, 0)
                gate_o(b, 1, 1)
                low_x(first)
                split_o(b, 1, 0)
                route(first, *range(10))
                residual_z(b, 1)
                route(first, *range(10, 16))

            def prepare_att(n, following):
                norm(n, "second")
                norm(n, 1)
                newton(n, *range(12))
                norm(n, 2)
                norm(n, 3)
                high_ax(n, 0)
                norm(following, 0)
                norm(following, 1)
                newton(following, 0, 1, 2)
                high_ax(n, 1)
                newton(following, *range(3, 12))

            def low_weight(k, dst, src, high, cut, copies):
                dve.wait_ge(copies_done, copies)
                v.tensor_tensor(dst[:, cut], src[:, cut], high[:, cut].bitcast(F32), ALU.subtract)\
                    .then_inc(w_split[k], 1)

            def start(first):
                v.memset(rw3[:], 0.0).then_inc(setup_done, 1)
                norm(first, 0)
                norm(first, 1)
                newton(first, *range(12))
                norm(first, 2)
                dve.wait_ge(w_loaded[0], 16)
                v.tensor_copy(ones[:], ones_f).then_inc(setup_done, 1)
                dve.wait_ge(w_loaded[1], 16)
                v.tensor_scalar(hb2[:], c(C_SB2), 0.5, None, ALU.mult).then_inc(setup_done, 1)
                low_x(first)
                low_weight(1, w3_l, stage[1], w3_h, FIRST, 2)
                low_weight(2, w1_l, stage[0], w1_h, FIRST, 3)
                low_weight(1, w3_l, stage[1], w3_h, REST, 4)
                route(first, 0, 1, 2)
                dve.wait_ge(stored[0], 16)
                v.tensor_copy(sel_sb[:], sel_f).then_inc(setup_done, 1)
                route(first, *range(3, 15))
                dve.wait_ge(setup_done, 1)
                route(first, 15)
                low_weight(2, w1_l, stage[0], w1_h, REST, 5)
                dve.wait_ge(stored[1], 16)
                dve.wait_ge(w_loaded[6], 32)
                v.tensor_copy(b2_h[:], b2_f)
                v.tensor_copy(bv_h[:], bv_f[:]).then_inc(setup_done, 1)
                dve.wait_ge(setup_done, 5)
                v.tensor_tensor(b2_lo[:], b2_f, b2_h[:].bitcast(F32), ALU.subtract).then_inc(setup_done, 1)
                v.tensor_tensor(bv_lo[:], bv_f[:], bv_h[:].bitcast(F32), ALU.subtract).then_inc(setup_done, 1)

            link_chunks_and_run(dve, ffn, residual, attention, attention_rest,
                                prepare_att=prepare_att, start=start)

        @block.gpsimd
        def _(pool):
            gp = nc.gpsimd

            def low(ch, j):
                n = ch.q * NBL + j
                pool.wait_ge(hi_done, (n + 1).value)
                gp.tensor_tensor(p_l[n.mod(4)][:], p[n.mod(2)][:], p_h[n.mod(4)][:].bitcast(F32),
                                 ALU.subtract).then_inc(lo_done, 1)

            def low_ax(n, h):
                pool.wait_ge(axh_done, (n.b * 2 + h + 1).value)
                gp.tensor_tensor(half(ax_l, h), axf[:], half(ax_h, h).bitcast(F32), ALU.subtract)\
                    .then_inc(axl_done, 1)

            def ffn(ch, before, pending, prep, att=None, following=None):
                for j in range(NBL):
                    if j >= 1:
                        low(ch, j - 1)
                    elif pending and before == "ffn":
                        low(ch.before, NBL - 1)
                    if prep and prep.kind == "att" and j in (6, 10):
                        low_ax(prep, j // 10)
                    if pending and before == "att" and j in (5, 6):
                        low_o(ch.att_b, 1, j - 5)

            def ffn_rest(ch):
                low(ch, NBL - 1)

            def low_o(b, h, k):
                pool.wait_ge(oh_done, (b * 2 + h + 1).value)
                gp.tensor_tensor(half(o_l, k), half(o_f, k), half(o_h, k).bitcast(F32), ALU.subtract)\
                    .then_inc(o_split, 1)

            def low_kq(b, k):
                pool.wait_ge(kq_hi, (b * 4 + k + 1).value)
                hi, lo = ((k_h, k_l), (q_h, q_l))[k % 2]
                gp.tensor_tensor(half(lo, k // 2), half(kqt, k % 2), half(hi, k // 2).bitcast(F32),
                                 ALU.subtract).then_inc(kq_lo, 1)

            def low_a(b, m):
                pool.wait_ge(ah_done, (b * (2 * KT) + m + 1).value)
                k = (m + 1) % 4
                gp.tensor_tensor(p_l[k][:], g[k][:], p_h[k][:].bitcast(F32), ALU.subtract).then_inc(al_done, 1)

            def attention(b, last_chunk, pending, prep):
                if pending:
                    low(last_chunk, NBL - 1)
                low_kq(b, 0)
                low_kq(b, 1)
                for m in range(2 * KT):
                    low_a(b, m)
                    if m == 0:
                        low_kq(b, 2)
                    if m == 3:
                        low_kq(b, 3)

            def attention_rest(b, first):
                low_o(b, 1, 0)
                low_o(b, 1, 1)

            def start(first):
                pool.wait_ge(copies_done, 1)
                gp.tensor_tensor(gw[:, E:], xb[:, O_GW:WS], ws_h[:, O_GW:].bitcast(F32), ALU.subtract)
                gp.tensor_tensor(ws_l[:], xb[:, 0:WS], ws_h[:].bitcast(F32), ALU.subtract).then_inc(w_split[0], 1)
                pool.wait_ge(copies_done, 6)
                gp.tensor_tensor(w2_l[:], stage[2], w2_h[:].bitcast(F32), ALU.subtract).then_inc(w_split[3], 1)

            link_chunks_and_run(pool, ffn, ffn_rest, attention, attention_rest,
                                prepare_att=lambda n, following: (low_ax(n, 0), low_ax(n, 1)), start=start)


PIECE = 4
FIRST, REST = slice(0, PIECE * P), slice(PIECE * P, HW)
SETUP = 7


def after_ffn(b):
    return b * (4 * NBL) + 2 * NBL


def ys_uses_before(b):
    return b * 4 + 2


def link_chunks_and_run(eng, ffn, ffn_rest, attention, attention_rest, prepare_att, start):
    def follow(n, before_kind, before):
        n.before_kind, n.before = before_kind, before
        return n

    c, first, second, att, following = phases_before()
    c[1].before = c[0]
    follow(first, None, None)
    follow(second, "ffn", Count(1))
    follow(att, "ffn", Count(2))
    follow(following, "att", Count(2))
    att.q_of_source = Count(1)
    c[0].norm, c[1].norm = first, second
    start(first)
    ffn(c[0], None, False, second)
    ffn(c[1], "ffn", True, None, att)
    ffn_rest(c[1])
    prepare_att(att, following)
    attention(Count(0), c[1], False, following)

    with eng.Fori(0, B - 1) as turn:
        c, preps, b, following = phases_of_turn(turn)
        for k in range(1, 4):
            c[k].before = c[k - 1]
        c[0].att_b = b - 1
        for k in range(4):
            follow(preps[k], "ffn", c[k].r + 1)
            c[k].norm = preps[k - 1]
        c[0].norm = Norm(None, None, "ffn", "xin", b, 0, c[0].r, c[0].q - 1)
        c[0].norm.after_att = True
        follow(following, "att", b * 2 + 2)
        preps[3].q_of_source = c[1].q
        ffn(c[0], "att", True, preps[0])
        for k in range(1, 4):
            ffn(c[k], "ffn", True, preps[k], preps[3] if k == 2 else None, following)
        attention(b, c[3], True, following)

    c, first, second = phases_after()
    c[0].att_b = Count(B - 1)
    c[1].before = c[0]
    follow(first, "ffn", c[0].q)
    follow(second, "ffn", c[1].q)
    attention_rest(Count(B - 1), first)
    c[0].norm, c[1].norm = first, second
    ffn(c[0], "att", False, second)
    ffn(c[1], "ffn", True, None)
    ffn_rest(c[1])


def kernel(L0_attn_x, L0_attn_ln_scale, L0_attn_ln_bias, L0_attn_W_hidden, L0_attn_b_hidden, L0_attn_W_qk,
           L0_attn_b_qk, L0_attn_os_weight, L0_attn_os_bias, L0_attn_W_out, L0_attn_b_out, L0_ffn_gate_w,
           L0_ffn_gate_b, L0_ffn_w1, L0_ffn_b1, L0_ffn_w3, L0_ffn_b3, L0_ffn_w2, L0_ffn_b2, L0_ffn_sw1,
           L0_ffn_sb1, L0_ffn_sw3, L0_ffn_sb3, L0_ffn_sw2, L0_ffn_sb2):
    import concourse.bacc as bacc
    from concourse.bass_utils import run_bass_kernel_spmd

    def arr(a):
        return np.ascontiguousarray(a)

    def blocks(flat):
        pad = np.zeros((HW - flat.shape[-1],), flat.dtype) if flat.ndim == 1 else \
            np.zeros((flat.shape[0], HW - flat.shape[-1]), flat.dtype)
        return np.concatenate([flat, pad], axis=-1)

    def mixed(w):
        w = arr(w)
        return w.reshape((E, NR, P // E) + w.shape[2:]).swapaxes(0, 1).reshape((E * H,) + w.shape[2:])

    def wide(w, sw):
        return blocks(np.concatenate([mixed(arr(w).transpose(0, 2, 1)).T, arr(sw)], axis=1))

    def by_block(b, sb):
        return blocks(np.concatenate([mixed(b), arr(sb)])).reshape(NBL, P).T

    down = np.concatenate([mixed(L0_ffn_w2), arr(L0_ffn_sw2)], axis=0)
    down = blocks(arr(down.T)).T.reshape(NBL, P, D).transpose(1, 0, 2).reshape(P, HW)
    osw, osb, bh = arr(L0_attn_os_weight), arr(L0_attn_os_bias), arr(L0_attn_b_hidden)
    one_cols = [L0_ffn_sb2, L0_attn_ln_scale, L0_attn_ln_bias, L0_attn_b_qk, bh[HID:HID + P], bh[HID + P:],
                osw[0], osw[1], osb[0], osb[1], L0_attn_b_out]
    cols = np.concatenate([by_block(L0_ffn_b1, L0_ffn_sb1), by_block(L0_ffn_b3, L0_ffn_sb3)]
                          + [arr(a).reshape(P, 1) for a in one_cols]
                          + [np.repeat(arr(L0_ffn_gate_b).reshape(1, E), P, axis=0)], axis=1)
    margin = np.triu(np.full((E, E), np.finfo(np.float32).tiny, np.float32)).reshape(1, E * E)
    consts = np.concatenate([np.eye(P, dtype=np.float32), np.repeat(margin, P, axis=0),
                             np.ones((P, P), np.float32)], axis=1)
    sel = np.repeat(np.tile(np.eye(E, dtype=np.float32), (2, 1)), P // E, axis=1)
    wo = arr(L0_attn_W_out).reshape(2, P, D).transpose(1, 0, 2).reshape(P, 2 * D)
    wsmall = np.concatenate([arr(L0_attn_W_hidden), arr(L0_attn_W_qk), wo, arr(L0_ffn_gate_w).T], axis=1)
    arrays = {
        "x": arr(L0_attn_x), "cols": arr(cols), "consts": arr(consts), "sel": arr(sel),
        "w1": arr(wide(L0_ffn_w1, L0_ffn_sw1)), "w3": arr(wide(L0_ffn_w3, L0_ffn_sw3)), "w2": arr(down),
        "wsmall": arr(wsmall), "b2": np.tile(arr(L0_ffn_b2), (3, 1)), "bv": arr(bh[:HID].reshape(1, HID)),
    }
    nc = bacc.Bacc("TRN2", target_bir_lowering=False, num_devices=1)
    args = [nc.dram_tensor(k, a.shape, mybir.dt.from_np(a.dtype), kind="ExternalInput").ap()
            for k, a in arrays.items()]
    out = nc.dram_tensor("out", (B, N, D), F32, kind="ExternalOutput").ap()
    build(nc, *args, out)
    got = run_bass_kernel_spmd(nc, [arrays], core_ids=[0])
    return got.results[0]["out"]
```
